# Optimizing a Trainium2 kernel written in Bass

```python
import numpy as np
import jax
import jax.numpy as jnp

def _softmax(x, axis=-1):
    return jax.nn.softmax(x, axis=axis)

def _gelu(x):
    return jax.nn.gelu(x, approximate=True)

def _silu(x):
    return jax.nn.silu(x)

def _sigmoid(x):
    return jax.nn.sigmoid(x)

def _layernorm(x, axis=-1, eps=1e-05):
    m = jnp.mean(x, axis=axis, keepdims=True)
    v = jnp.var(x, axis=axis, keepdims=True)
    return (x - m) / jnp.sqrt(v + eps)

def _scatter_add(tgt, idx, src, axis=0):
    return tgt.at[idx].add(src)

def _segment_sum(src, seg, n):
    return jax.ops.segment_sum(src, seg, n)
kernel_name = 'mk_gnn_resnorm_d4_gnn_r32_3c4e80'

def setup_inputs(seed: int=0):
    np.random.seed(seed)
    _w = jnp.asarray

    def _rec_inputs():
        import jax
        import jax.numpy as jnp
        _gk = jax.random.key(seed)
        x = -0.0005121 + 1.001 * jax.random.normal(jax.random.fold_in(_gk, 1), (3125, 64), jnp.float32)
        src = jax.random.randint(jax.random.fold_in(_gk, 2), (100000,), 0, 3125, jnp.int32)
        dst = jnp.minimum((3125 * jax.random.uniform(jax.random.fold_in(_gk, 3), (100000,)) ** 2.0).astype(jnp.int32), 99999)
        _o = jnp.argsort(dst, stable=True)
        src = src[_o]
        dst = dst[_o]
        edge_type_8 = jax.random.randint(jax.random.fold_in(_gk, 13), (100000,), 0, 8, jnp.int32)
        edge_weight = jax.random.uniform(jax.random.fold_in(_gk, 14), (100000,), jnp.float32, 0.0, 0.999999)
        edge_weight_n2 = jax.random.uniform(jax.random.fold_in(_gk, 15), (100000,), jnp.float32, 0.0, 0.999999)
        return (x, src, dst, edge_type_8, edge_weight, edge_weight_n2)
    x, src, dst, edge_type_8, edge_weight, edge_weight_n2 = _rec_inputs()

    def _L0_gnn_setup():
        import jax, jax.numpy as jnp
        import numpy as np
        N = 50000
        E = 12500
        F_IN = 64
        HID = 128
        OUT = 64
        HEADS = 4
        NEG_SLOPE = 0.2
        BN_EPS = 1e-05

        def _gat_conv(x, src, dst, W, a_src, a_dst, bias, heads, ch):
            n = x.shape[0]
            h = (x @ W).reshape(n, heads, ch)
            alpha_src = jnp.sum(h * a_src, axis=-1)
            alpha_dst = jnp.sum(h * a_dst, axis=-1)
            e = jax.nn.leaky_relu(alpha_src[src] + alpha_dst[dst], NEG_SLOPE)
            m = jax.lax.stop_gradient(jax.ops.segment_max(e, dst, num_segments=n))
            ex = jnp.exp(e - m[dst])
            den = jax.ops.segment_sum(ex, dst, num_segments=n)
            alpha = ex / den[dst]
            msg = h[src] * alpha[..., None]
            out = jax.ops.segment_sum(msg, dst, num_segments=n)
            return jnp.mean(out, axis=1) + bias

        def _batch_norm(x, gamma, beta):
            mu = jnp.mean(x, axis=0)
            var = jnp.mean(jnp.square(x - mu), axis=0)
            return (x - mu) * jax.lax.rsqrt(var + BN_EPS) * gamma + beta
        key = jax.random.key(seed)
        ks = jax.random.split(key, 20)
        f = lambda k, shape, s=0.1: jax.random.normal(k, shape, jnp.float32) * s
        return {'x': jax.random.normal(ks[0], (N, F_IN), jnp.float32), 'edge_index': jax.random.randint(ks[1], (2, E), 0, N, jnp.int32), 'W1': f(ks[2], (F_IN, HEADS * HID)), 'as1': f(ks[3], (HEADS, HID)), 'ad1': f(ks[4], (HEADS, HID)), 'b1': f(ks[5], (HID,)), 'g1': jnp.ones((HID,), jnp.float32), 'be1': jnp.zeros((HID,), jnp.float32), 'W2': f(ks[6], (HID, HEADS * HID)), 'as2': f(ks[7], (HEADS, HID)), 'ad2': f(ks[8], (HEADS, HID)), 'b2': f(ks[9], (HID,)), 'g2': jnp.ones((HID,), jnp.float32), 'be2': jnp.zeros((HID,), jnp.float32), 'W3': f(ks[10], (HID, 1 * OUT)), 'as3': f(ks[11], (1, OUT)), 'ad3': f(ks[12], (1, OUT)), 'b3': f(ks[13], (OUT,))}
    _L0_gnn_all = _L0_gnn_setup()
    _L0_gnn_in = {k: v for k, v in _L0_gnn_all.items() if k in ('W1', 'as1', 'ad1', 'b1', 'g1', 'be1', 'W2', 'as2', 'ad2', 'b2', 'g2', 'be2', 'W3', 'as3', 'ad3', 'b3')}
    del _L0_gnn_all

    def _L1_gnn_setup():
        import jax, jax.numpy as jnp
        import numpy as np
        N_NODES = 3125
        N_EDGES = 50000
        D = 64
        N_LAYERS = 3
        key = jax.random.key(seed)
        k1, k2, k3, k4 = jax.random.split(key, 4)
        x = jax.random.normal(k1, (N_NODES, D), dtype=jnp.float32)
        edge_index = jax.random.randint(k2, (2, N_EDGES), 0, N_NODES, dtype=jnp.int64)
        scale = 1.0 / np.sqrt(D)
        W_self = jax.random.normal(k3, (N_LAYERS, D, D), dtype=jnp.float32) * scale
        W_neigh = jax.random.normal(k4, (N_LAYERS, D, D), dtype=jnp.float32) * scale
        b = jnp.zeros((N_LAYERS, D), dtype=jnp.float32)
        return {'x': x, 'edge_index': edge_index, 'W_self': W_self, 'W_neigh': W_neigh, 'b': b}
    _L1_gnn_all = _L1_gnn_setup()
    _L1_gnn_in = {k: v for k, v in _L1_gnn_all.items() if k in ('W_self', 'W_neigh', 'b')}
    del _L1_gnn_all

    def _L2_gnn_setup():
        import jax, jax.numpy as jnp
        import numpy as np
        N_NODES = 3125
        N_EDGES = 40000
        HID = 64
        MSG = 64
        N_ETYPE = 8

        def _ggnn_forward(h, edge_matrix, w_ih, w_hh, b_ih, b_hh, edge_src, edge_dst, edge_type):
            N, H = h.shape
            T = edge_matrix.shape[0]
            M = edge_matrix.shape[1] // H
            A = edge_matrix.reshape(T, M, H)
            Ht = jnp.einsum('tmh,nh->tnm', A, h)
            msg = Ht[edge_type, edge_src]
            m_agg = jax.ops.segment_sum(msg, edge_dst, num_segments=N)
            gi = m_agg @ w_ih.T + b_ih
            gh = h @ w_hh.T + b_hh
            i_r, i_z, i_n = (gi[:, :H], gi[:, H:2 * H], gi[:, 2 * H:])
            h_r, h_z, h_n = (gh[:, :H], gh[:, H:2 * H], gh[:, 2 * H:])
            r = jax.nn.sigmoid(i_r + h_r)
            z = jax.nn.sigmoid(i_z + h_z)
            n = jnp.tanh(i_n + r * h_n)
            return (1.0 - z) * n + z * h
        key = jax.random.key(seed)
        ks = jax.random.split(key, 9)
        s = 1.0 / np.sqrt(HID)
        return {'h': jax.random.normal(ks[0], (N_NODES, HID), jnp.float32) * s, 'edge_matrix': jax.random.normal(ks[1], (N_ETYPE, MSG * HID), jnp.float32) * s, 'w_ih': jax.random.normal(ks[2], (3 * HID, MSG), jnp.float32) * s, 'w_hh': jax.random.normal(ks[3], (3 * HID, HID), jnp.float32) * s, 'b_ih': jax.random.normal(ks[4], (3 * HID,), jnp.float32) * s, 'b_hh': jax.random.normal(ks[5], (3 * HID,), jnp.float32) * s, 'edge_src': jax.random.randint(ks[6], (N_EDGES,), 0, N_NODES, jnp.int32), 'edge_dst': jax.random.randint(ks[7], (N_EDGES,), 0, N_NODES, jnp.int32), 'edge_type': jax.random.randint(ks[8], (N_ETYPE if False else N_EDGES,), 0, N_ETYPE, jnp.int32)}
    _L2_gnn_all = _L2_gnn_setup()
    _L2_gnn_in = {k: v for k, v in _L2_gnn_all.items() if k in ('edge_matrix', 'w_ih', 'w_hh', 'b_ih', 'b_hh')}
    del _L2_gnn_all

    def _L3_gnn_setup():
        import jax, jax.numpy as jnp
        import numpy as np
        N, E, D_IN, D_OUT = (2048, 32768, 64, 64)
        EPS = 1e-08
        key = jax.random.key(seed)
        ks = jax.random.split(key, 8)
        h = jax.random.normal(ks[0], (N, D_IN), dtype=jnp.float32)
        edge_index = jax.random.randint(ks[1], (2, E), 0, N, dtype=jnp.int64 if jax.config.jax_enable_x64 else jnp.int32)
        adj_v = jax.random.uniform(ks[2], (E,), dtype=jnp.float32)
        deg_v = jax.random.uniform(ks[3], (E,), dtype=jnp.float32)
        W = jax.random.normal(ks[4], (D_IN, D_OUT), dtype=jnp.float32) / np.sqrt(D_IN)
        b = jax.random.normal(ks[5], (D_OUT,), dtype=jnp.float32) * 0.01
        deg_coeff = jnp.array([0.5, 0.0], dtype=jnp.float32)
        coeff_param = jnp.zeros((3,), dtype=jnp.float32)
        scale_param = 2.0 * jnp.ones((1,), dtype=jnp.float32)
        return {'h': h, 'edge_index': edge_index, 'adj_v': adj_v, 'deg_v': deg_v, 'W': W, 'b': b, 'deg_coeff': deg_coeff, 'coeff_param': coeff_param, 'scale_param': scale_param}
    _L3_gnn_all = _L3_gnn_setup()
    _L3_gnn_in = {k: v for k, v in _L3_gnn_all.items() if k in ('W', 'b', 'deg_coeff', 'coeff_param', 'scale_param')}
    del _L3_gnn_all
    return {'x': x, 'src': src, 'dst': dst, 'edge_type_8': edge_type_8, 'edge_weight': edge_weight, 'edge_weight_n2': edge_weight_n2, 'L0_gnn_W1': _L0_gnn_in['W1'], 'L0_gnn_as1': _L0_gnn_in['as1'], 'L0_gnn_ad1': _L0_gnn_in['ad1'], 'L0_gnn_b1': _L0_gnn_in['b1'], 'L0_gnn_g1': _L0_gnn_in['g1'], 'L0_gnn_be1': _L0_gnn_in['be1'], 'L0_gnn_W2': _L0_gnn_in['W2'], 'L0_gnn_as2': _L0_gnn_in['as2'], 'L0_gnn_ad2': _L0_gnn_in['ad2'], 'L0_gnn_b2': _L0_gnn_in['b2'], 'L0_gnn_g2': _L0_gnn_in['g2'], 'L0_gnn_be2': _L0_gnn_in['be2'], 'L0_gnn_W3': _L0_gnn_in['W3'], 'L0_gnn_as3': _L0_gnn_in['as3'], 'L0_gnn_ad3': _L0_gnn_in['ad3'], 'L0_gnn_b3': _L0_gnn_in['b3'], 'L1_gnn_W_self': _L1_gnn_in['W_self'], 'L1_gnn_W_neigh': _L1_gnn_in['W_neigh'], 'L1_gnn_b': _L1_gnn_in['b'], 'L2_gnn_edge_matrix': _L2_gnn_in['edge_matrix'], 'L2_gnn_w_ih': _L2_gnn_in['w_ih'], 'L2_gnn_w_hh': _L2_gnn_in['w_hh'], 'L2_gnn_b_ih': _L2_gnn_in['b_ih'], 'L2_gnn_b_hh': _L2_gnn_in['b_hh'], 'L3_gnn_W': _L3_gnn_in['W'], 'L3_gnn_b': _L3_gnn_in['b'], 'L3_gnn_deg_coeff': _L3_gnn_in['deg_coeff'], 'L3_gnn_coeff_param': _L3_gnn_in['coeff_param'], 'L3_gnn_scale_param': _L3_gnn_in['scale_param']}

def reference(x, src, dst, edge_type_8, edge_weight, edge_weight_n2, L0_gnn_W1, L0_gnn_as1, L0_gnn_ad1, L0_gnn_b1, L0_gnn_g1, L0_gnn_be1, L0_gnn_W2, L0_gnn_as2, L0_gnn_ad2, L0_gnn_b2, L0_gnn_g2, L0_gnn_be2, L0_gnn_W3, L0_gnn_as3, L0_gnn_ad3, L0_gnn_b3, L1_gnn_W_self, L1_gnn_W_neigh, L1_gnn_b, L2_gnn_edge_matrix, L2_gnn_w_ih, L2_gnn_w_hh, L2_gnn_b_ih, L2_gnn_b_hh, L3_gnn_W, L3_gnn_b, L3_gnn_deg_coeff, L3_gnn_coeff_param, L3_gnn_scale_param):
    import jax
    import jax.numpy as jnp

    def _L0_gnn_ref(x, edge_index, W1, as1, ad1, b1, g1, be1, W2, as2, ad2, b2, g2, be2, W3, as3, ad3, b3):
        import jax, jax.numpy as jnp
        import numpy as np
        N = 50000
        E = 12500
        F_IN = 64
        HID = 128
        OUT = 64
        HEADS = 4
        NEG_SLOPE = 0.2
        BN_EPS = 1e-05

        def _gat_conv(x, src, dst, W, a_src, a_dst, bias, heads, ch):
            n = x.shape[0]
            h = (x @ W).reshape(n, heads, ch)
            alpha_src = jnp.sum(h * a_src, axis=-1)
            alpha_dst = jnp.sum(h * a_dst, axis=-1)
            e = jax.nn.leaky_relu(alpha_src[src] + alpha_dst[dst], NEG_SLOPE)
            m = jax.lax.stop_gradient(jax.ops.segment_max(e, dst, num_segments=n))
            ex = jnp.exp(e - m[dst])
            den = jax.ops.segment_sum(ex, dst, num_segments=n)
            alpha = ex / den[dst]
            msg = h[src] * alpha[..., None]
            out = jax.ops.segment_sum(msg, dst, num_segments=n)
            return jnp.mean(out, axis=1) + bias

        def _batch_norm(x, gamma, beta):
            mu = jnp.mean(x, axis=0)
            var = jnp.mean(jnp.square(x - mu), axis=0)
            return (x - mu) * jax.lax.rsqrt(var + BN_EPS) * gamma + beta
        n = x.shape[0]
        loop = jnp.arange(n, dtype=edge_index.dtype)
        src = jnp.concatenate([edge_index[0], loop])
        dst = jnp.concatenate([edge_index[1], loop])
        h = _gat_conv(x, src, dst, W1, as1, ad1, b1, HEADS, HID)
        h = jax.nn.elu(_batch_norm(h, g1, be1))
        h = _gat_conv(h, src, dst, W2, as2, ad2, b2, HEADS, HID)
        h = jax.nn.elu(_batch_norm(h, g2, be2))
        return _gat_conv(h, src, dst, W3, as3, ad3, b3, 1, OUT)

    def _L1_gnn_ref(x, edge_index, W_self, W_neigh, b):
        import jax, jax.numpy as jnp
        import numpy as np
        N_NODES = 3125
        N_EDGES = 50000
        D = 64
        N_LAYERS = 3
        n = x.shape[0]
        src = edge_index[0]
        dst = edge_index[1]
        deg = jax.ops.segment_sum(jnp.ones((src.shape[0],), x.dtype), dst, num_segments=n)
        inv_deg = jnp.where(deg > 0, 1.0 / jnp.maximum(deg, 1.0), 0.0)[:, None]

        def sage_conv(h, ws, wn, bb):
            agg = jax.ops.segment_sum(h[src], dst, num_segments=n) * inv_deg
            return h @ ws + agg @ wn + bb
        h = x
        for l in range(N_LAYERS):
            h = sage_conv(h, W_self[l], W_neigh[l], b[l])
            if l < N_LAYERS - 1:
                h = jax.nn.relu(h)
        return h

    def _L2_gnn_ref(h, edge_matrix, w_ih, w_hh, b_ih, b_hh, edge_src, edge_dst, edge_type):
        import jax, jax.numpy as jnp
        import numpy as np
        N_NODES = 3125
        N_EDGES = 40000
        HID = 64
        MSG = 64
        N_ETYPE = 8

        def _ggnn_forward(h, edge_matrix, w_ih, w_hh, b_ih, b_hh, edge_src, edge_dst, edge_type):
            N, H = h.shape
            T = edge_matrix.shape[0]
            M = edge_matrix.shape[1] // H
            A = edge_matrix.reshape(T, M, H)
            Ht = jnp.einsum('tmh,nh->tnm', A, h)
            msg = Ht[edge_type, edge_src]
            m_agg = jax.ops.segment_sum(msg, edge_dst, num_segments=N)
            gi = m_agg @ w_ih.T + b_ih
            gh = h @ w_hh.T + b_hh
            i_r, i_z, i_n = (gi[:, :H], gi[:, H:2 * H], gi[:, 2 * H:])
            h_r, h_z, h_n = (gh[:, :H], gh[:, H:2 * H], gh[:, 2 * H:])
            r = jax.nn.sigmoid(i_r + h_r)
            z = jax.nn.sigmoid(i_z + h_z)
            n = jnp.tanh(i_n + r * h_n)
            return (1.0 - z) * n + z * h
        return _ggnn_forward(h, edge_matrix, w_ih, w_hh, b_ih, b_hh, edge_src, edge_dst, edge_type)

    def _L3_gnn_ref(h, edge_index, adj_v, deg_v, W, b, deg_coeff, coeff_param, scale_param):
        import jax, jax.numpy as jnp
        import numpy as np
        N, E, D_IN, D_OUT = (2048, 32768, 64, 64)
        EPS = 1e-08
        n_nodes = h.shape[0]
        Wh = h @ W + b
        row, col = (edge_index[0], edge_index[1])
        sc = jax.nn.softplus(deg_coeff[0] * deg_v + deg_coeff[1])
        Wr = Wh[row]
        Wc = Wh[col]
        dot = jnp.sum(Wr * Wc, axis=-1)
        nr = jnp.sqrt(jnp.sum(Wr * Wr, axis=-1))
        nc = jnp.sqrt(jnp.sum(Wc * Wc, axis=-1))
        sim = dot / jnp.maximum(nr * nc, EPS)
        sim_pos = jax.nn.relu(sim)
        sim_neg = -jax.nn.relu(-sim)
        no_diag = (row != col).astype(Wh.dtype)
        base = adj_v * sc * no_diag
        prop_pos = jax.ops.segment_sum((base * sim_pos)[:, None] * Wc, row, num_segments=n_nodes)
        prop_neg = jax.ops.segment_sum((base * sim_neg)[:, None] * Wc, row, num_segments=n_nodes)
        coeff = jax.nn.softmax(coeff_param)
        scale = jax.nn.softplus(scale_param)
        return scale * (coeff[0] * prop_pos + coeff[1] * prop_neg + coeff[2] * Wh)
    edge_index = jnp.stack([src, dst])
    x = _layernorm(x + _L0_gnn_ref(x, edge_index, L0_gnn_W1, L0_gnn_as1, L0_gnn_ad1, L0_gnn_b1, L0_gnn_g1, L0_gnn_be1, L0_gnn_W2, L0_gnn_as2, L0_gnn_ad2, L0_gnn_b2, L0_gnn_g2, L0_gnn_be2, L0_gnn_W3, L0_gnn_as3, L0_gnn_ad3, L0_gnn_b3), axis=-1)
    x = _layernorm(x + _L1_gnn_ref(x, edge_index, L1_gnn_W_self, L1_gnn_W_neigh, L1_gnn_b), axis=-1)
    x = _layernorm(x + _L2_gnn_ref(x, L2_gnn_edge_matrix, L2_gnn_w_ih, L2_gnn_w_hh, L2_gnn_b_ih, L2_gnn_b_hh, src, dst, edge_type_8), axis=-1)
    x = _layernorm(x + _L3_gnn_ref(x, edge_index, edge_weight, edge_weight_n2, L3_gnn_W, L3_gnn_b, L3_gnn_deg_coeff, L3_gnn_coeff_param, L3_gnn_scale_param), axis=-1)
    return x

_drawn_inputs = setup_inputs


def setup_inputs(seed=0):
    import zlib

    import numpy as np

    out = dict(_drawn_inputs(seed))
    spreads = {'L0_gnn_g1': (1.0, 0.2),
     'L0_gnn_be1': (0.0, 0.799),
     'L0_gnn_g2': (1.0, 0.2),
     'L0_gnn_be2': (0.0, 0.1),
     'L1_gnn_b': (0.0, 0.1),
     'L3_gnn_coeff_param': (0.0, 0.1)}
    factors = {'edge_weight_n2': 2.689,
     'L0_gnn_b1': 8.0,
     'L0_gnn_b2': 8.0,
     'L2_gnn_b_ih': 3.997,
     'L2_gnn_b_hh': 5.682,
     'L3_gnn_b': 3.418}
    for name, (base, spread) in spreads.items():
        noise = np.random.default_rng([zlib.crc32(name.encode()), seed]).standard_normal(out[name].shape)
        drawn = base * np.exp(spread * noise) if base else spread * noise
        out[name] = jnp.asarray(drawn.astype(out[name].dtype))
    for name, factor in factors.items():
        out[name] = (out[name] * factor).astype(out[name].dtype)
    return out
```

```python
import numpy as np
import concourse.bass as bass
from concourse import mybir
from concourse.alu_op_type import AluOpType as ALU

ACT = mybir.ActivationFunctionType
AX = mybir.AxisListType.X
F32 = mybir.dt.float32
I32 = mybir.dt.int32
RMAX = bass.bass_isa.ReduceOp.max
ds = bass.ds

P = 125
N = 3125
NW = N // P
E = 100000
C = E // P
G = 8
T = 832
NG = T // G
SG = T // 8
D = 64
NT = 8
ROUND = 12582912.0
LN_EPS = 1e-5
BN_EPS = 1e-5
SIM_EPS = 1e-8
SLOPE = 0.2


class Counted:

    def __init__(self, nc, ctx, name):
        self.sem = ctx.enter_context(nc.semaphore(name))
        self.n = 0


def gnn_kernel(nc, x_in, src_in, dst_in, type_in, w1_in, w2_in,
               W1, as1, ad1, b1, g1, be1, W2, as2, ad2, b2, g2, be2, W3, as3, ad3, b3,
               W_self, W_neigh, b_sage, edge_matrix, w_ih, w_hh, b_ih, b_hh,
               W_cos, b_cos, deg_coeff, coeff_param, scale_param, out):
    from contextlib import ExitStack
    ctx = ExitStack()
    with ctx:
        ctx.enter_context(nc.allow_non_contiguous_dma(reason="one column of small tables"))

        def sb(name, shape, dt=F32):
            return ctx.enter_context(nc.sbuf_tensor(name, shape, dt))

        def dram(name, shape, dt=F32):
            return nc.dram_tensor(name, shape, dt, kind="Internal").ap()

        def sem(name):
            return ctx.enter_context(nc.semaphore(name))

        dloc = sb("dloc", [P, T])
        src_hi = sb("src_hi", [P, T])
        src_lo = sb("src_lo", [P, T])
        base_w = sb("base_w", [P, T])
        src_idx = sb("src_idx", [P, T + G], I32)
        typed_idx = sb("typed_idx", [P, T + G], I32)
        win_row = sb("win_row", [1, T], I32)
        acc = sb("acc", [P, NW * 517])
        arena = sb("arena", [128, 4 * N])
        gath = sb("gath", [P, 4, G, 132])
        onehot = sb("onehot", [P, 4, G, P])
        group_idx = sb("group_idx", [P, 4, G], I32)
        x = sb("x", [P, NW, D])
        h = sb("h", [P, NW, 128])
        tmp = sb("tmp", [128, NW * 128])
        iota_row = sb("iota_row", [P, P])
        ident = sb("ident", [128, 128])
        ones = sb("ones", [P, P])
        alpha = sb("alpha", [P, NW, 8])
        alpha_win = sb("alpha_win", [P, NW * 4])
        alpha_max = sb("alpha_max", [P, 4])
        inv_deg = sb("inv_deg", [P, NW])
        wts = sb("wts", [128, 512])
        watt = sb("watt", [128, 8])
        vecs = sb("vecs", [P, 1024])
        stat = sb("stat", [P, 4, 128])
        small = sb("small", [P, 8, NW])
        slotv = sb("slotv", [P, 16, G * 4])
        ps = ctx.enter_context(nc.psum_tensor("ps", [128, 8, 512], F32))

        xT = arena[:, 0:N]
        tT = [arena[:, i * N:(i + 1) * N] for i in range(4)]

        win_tab = dram("win_tab", [T], I32)
        tab = {}

        dma = Counted(nc, ctx, "dma_done")
        chain = Counted(nc, ctx, "vector_chain")
        node_mm = Counted(nc, ctx, "node_products_ready")
        node_ev = Counted(nc, ctx, "node_products_read")
        act_ch = Counted(nc, ctx, "scalar_chain")
        pool_ch = Counted(nc, ctx, "pool_chain")

        def link(eng, ins, counted=chain):
            counted.n += 1
            ins.then_inc(counted.sem, 1)
            eng.wait_ge(counted.sem, counted.n)

        def copies(*pairs):
            with nc.Block() as block:
                @block.sync
                def _(sp):
                    for dst_ap, src_ap in pairs:
                        sp.dma_start(dst_ap, src_ap).then_inc(dma.sem, 16)
                        dma.n += 16
                    sp.wait_ge(dma.sem, dma.n)

        def row(ap, parts=P):
            return ap.unsqueeze(0).to_broadcast([parts, ap.shape[0]])

        def bw(ap, width=None):
            return ap.unsqueeze(1).to_broadcast([ap.shape[0], NW, ap.shape[-1]])

        def bf(ap, n):
            return ap.unsqueeze(len(ap.shape)).to_broadcast([*ap.shape, n])

        def scalar_fn(out_ap, in_ap, fn, **kw):
            with nc.Block() as block:
                @block.scalar
                def _(act):
                    nc.scalar.activation(out_ap, in_ap, fn, **kw)

        def vector_block(body):
            with nc.Block() as block:
                @block.vector
                def _(dve):
                    body(nc.vector, lambda ins: link(dve, ins))

        def node_transpose(jobs):
            rounds = [(s, f, d, w) for s, f, d in jobs for w in range(0, NW, 4)]
            m0, e0 = node_mm.n, node_ev.n
            with nc.Block() as block:
                @block.tensor
                def _(pe):
                    for r, (s, f, d, w0) in enumerate(rounds):
                        if r >= 8:
                            pe.wait_ge(node_ev.sem, e0 + r - 7)
                        for k, w in enumerate(range(w0, min(w0 + 4, NW))):
                            last = nc.tensor.transpose(ps[0:f, r % 8, k * P:(k + 1) * P], s(w), ident[0:P, 0:P])
                        last.then_inc(node_mm.sem, 1)

                @block.vector
                def _(dve):
                    for r, (s, f, d, w0) in enumerate(rounds):
                        n = (min(w0 + 4, NW) - w0) * P
                        dve.wait_ge(node_mm.sem, m0 + r + 1)
                        nc.vector.tensor_copy(d[0:f, w0 * P:w0 * P + n], ps[0:f, r % 8, 0:n]).then_inc(node_ev.sem, 1)
            node_mm.n += len(rounds)
            node_ev.n += len(rounds)

        def node_matmul(terms, width, read):
            per = min(4, 512 // width)
            rounds = list(range(0, NW, per))
            m0, e0 = node_mm.n, node_ev.n
            with nc.Block() as block:
                @block.tensor
                def _(pe):
                    for r, w0 in enumerate(rounds):
                        if r >= 8:
                            pe.wait_ge(node_ev.sem, e0 + r - 7)
                        for k, w in enumerate(range(w0, min(w0 + per, NW))):
                            for i, (lhsT, rhs) in enumerate(terms):
                                last = nc.tensor.matmul(ps[0:P, r % 8, k * width:(k + 1) * width], lhsT(w), rhs,
                                                        start=(i == 0), stop=(i == len(terms) - 1))
                        last.then_inc(node_mm.sem, 1)

                @block.vector
                def _(dve):
                    for r, w0 in enumerate(rounds):
                        n = min(w0 + per, NW) - w0
                        dve.wait_ge(node_mm.sem, m0 + r + 1)
                        v = ps[0:P, r % 8, 0:n * width].rearrange("p (k c) -> p k c", c=width)
                        read(v, w0, n).then_inc(node_ev.sem, 1)
            node_mm.n += len(rounds)
            node_ev.n += len(rounds)

        def window_of(t, f):
            return lambda w: t[0:f, w * P:(w + 1) * P]

        def column_sums(table, out_ap):
            m0 = node_mm.n
            with nc.Block() as block:
                @block.tensor
                def _(pe):
                    for w in range(NW):
                        last = nc.tensor.matmul(ps[0:P, 0, 0:128], ones[:, :], table(w), start=(w == 0), stop=(w == NW - 1))
                    last.then_inc(node_mm.sem, 1)

                @block.vector
                def _(dve):
                    dve.wait_ge(node_mm.sem, m0 + 1)
                    nc.vector.tensor_copy(out_ap, ps[0:P, 0, 0:128])
            node_mm.n += 1

        def layernorm(t):
            sq = tmp[0:P, 0:NW * D].rearrange("p (w f) -> p w f", f=D)

            def centre(v, ln):
                ln(v.tensor_reduce(small[:, 0, :], t, AX, ALU.add))
                ln(v.tensor_scalar(small[:, 0, :], small[:, 0, :], 1.0 / D, None, ALU.mult))
                ln(v.tensor_tensor(t, t, bf(small[:, 0, :], D), ALU.subtract))
                ln(v.tensor_tensor(sq, t, t, ALU.mult))
                ln(v.tensor_reduce(small[:, 1, :], sq, AX, ALU.add))
                v.tensor_scalar(small[:, 1, :], small[:, 1, :], 1.0 / D, LN_EPS, ALU.mult, ALU.add)
            vector_block(centre)
            scalar_fn(small[:, 2, :], small[:, 1, :], ACT.Sqrt)

            def scale(v, ln):
                ln(v.reciprocal(small[:, 3, :], small[:, 2, :]))
                v.tensor_tensor(t, t, bf(small[:, 3, :], D), ALU.mult)
            vector_block(scale)

        lastd = tmp[0:1, 0:C].bitcast(I32)
        lastw = tmp[0:1, C:2 * C]
        ciota = sb("ciota", [1, C], I32)
        tcol = sb("tcol", [SG, 8], I32)
        slot_c = sb("slot_c", [SG, 8])
        slot_w = sb("slot_w", [SG, 8])
        slot_t = sb("slot_t", [SG, 8])
        slot_ci = sb("slot_ci", [SG, 8], I32)
        slot_wi = sb("slot_wi", [SG, 8], I32)
        iota_i = arena[0:P, 0:P].bitcast(I32)
        dcol = sb("dcol", [SG, 2])
        raw = acc[0:SG, 0:5 * 1000].rearrange("p (a n) -> p a n", a=5)
        A = [acc[0:SG, 5000 + k * 1000:6000 + k * 1000] for k in range(7)]
        S, Dst, Ty, shi_s, slo_s, val_s, base_s = A
        U = [tmp[0:SG, k * 1000:(k + 1) * 1000] for k in range(3)]

        copies((lastd, dst_in.rearrange("(c e) -> c e", e=P)[:, P - 1:P].rearrange("c e -> e c")),
               (x[:, :, :], x_in.rearrange("(w p) f -> p w f", p=P)),
               (dcol[:, :], row(deg_coeff, SG)))
        with nc.Block() as block:
            @block.gpsimd
            def _(pool):
                nc.gpsimd.iota(iota_i, [[1, P]], base=0, channel_multiplier=0)
                nc.gpsimd.iota(ciota[:, :], [[1, C]], base=0, channel_multiplier=0)
                nc.gpsimd.iota(tcol[:, :], [[SG, 8]], base=0, channel_multiplier=1)
                link(pool, nc.gpsimd.memset(ident[:, :], 0.0), pool_ch)
                nc.gpsimd.affine_select(out=ident[:, :], in_=ident[:, :], compare_op=ALU.not_equal, fill=1.0,
                                        base=0, pattern=[[-1, 128]], channel_multiplier=1)
                nc.gpsimd.memset(ones[:, :], 1.0)

        def last_windows(v, ln):
            v.tensor_copy(iota_row[:, :], iota_i)
            v.tensor_copy(slot_t[:, :], tcol[:, :])
            ln(v.tensor_copy(lastw, lastd))
            ln(v.tensor_scalar(lastw, lastw, -float(P // 2), 1.0 / P, ALU.add, ALU.mult))
            ln(v.tensor_scalar(lastw, lastw, ROUND, ROUND, ALU.add, ALU.subtract))
            v.tensor_tensor(lastw, lastw, ciota[:, :], ALU.add)
        vector_block(last_windows)
        with nc.Block() as block:
            @block.tensor
            def _(pe):
                for k in range(2):
                    nc.tensor.matmul(ps[0:SG, k, 0:C // 2], ones[0:1, 0:SG], lastw[:, k * (C // 2):(k + 1) * (C // 2)],
                                     start=True, stop=True)

        def slots(v, ln):
            for g in range(8):
                c = U[g % 3][:, 0:C]
                ln(v.tensor_scalar(c.rearrange("p (k n) -> p k n", k=2), ps[0:SG, 0:2, 0:C // 2],
                                   slot_t[:, g:g + 1], None, ALU.is_lt))
                ln(v.tensor_reduce(slot_c[:, g:g + 1], c, AX, ALU.add))
            ln(v.tensor_scalar(slot_c[:, :], slot_c[:, :], float(C - 1), None, ALU.min))
            ln(v.tensor_copy(slot_ci[:, :], slot_c[:, :]))
            ln(v.tensor_tensor(slot_w[:, :], slot_t[:, :], slot_c[:, :], ALU.subtract))
            ln(v.tensor_scalar(slot_wi[:, :], slot_w[:, :], float(NW - 1), None, ALU.min))
            v.tensor_scalar(slot_w[:, :], slot_w[:, :], float(P), None, ALU.mult)
        vector_block(slots)
        slots_in = sem("slots_gathered")
        with nc.Block() as block:
            @block.sync
            def _(sp):
                sp.dma_start(win_tab.rearrange("(g p) -> p g", p=SG), slot_wi[:, :]).then_inc(dma.sem, 16)
                sp.wait_ge(dma.sem, dma.n + 16)
                sp.dma_start(win_row[:, :], win_tab.unsqueeze(0)).then_inc(dma.sem, 16)
                sp.wait_ge(dma.sem, dma.n + 32)

            @block.gpsimd
            def _(pool):
                k = 0
                for a, t in enumerate((src_in, dst_in, type_in, w1_in, w2_in)):
                    v = t.rearrange("(c e) -> c e", e=P)
                    for g in range(8):
                        o = raw[:, a, g * P:(g + 1) * P]
                        nc.gpsimd.indirect_dma_start(o if a > 2 else o.bitcast(I32), None, v,
                                                     bass.IndirectOffsetOnAxis(ap=slot_ci[:, g:g + 1], axis=0)
                                                     ).then_inc(slots_in, 16)
                        k += 16
                pool.wait_ge(slots_in, k)
        dma.n += 32

        def g3(ap):
            return ap.rearrange("p (g e) -> p g e", e=P)

        def edges1(v, ln):
            ln(v.tensor_copy(S, raw[:, 0, :].bitcast(I32)))
            ln(v.tensor_copy(Dst, raw[:, 1, :].bitcast(I32)))
            ln(v.tensor_copy(Ty, raw[:, 2, :].bitcast(I32)))
            ln(v.tensor_tensor(val_s, S, Dst, ALU.not_equal))
            ln(v.tensor_tensor(g3(Dst), g3(Dst), bf(slot_w[:, :], P), ALU.subtract))
            ln(v.scalar_tensor_tensor(val_s, Dst, 0.0, val_s, ALU.is_ge, ALU.mult))
            ln(v.scalar_tensor_tensor(val_s, Dst, float(P - 1), val_s, ALU.is_le, ALU.mult))
            ln(v.scalar_tensor_tensor(Ty, S, float(NT), Ty, ALU.mult, ALU.add))
            ln(v.tensor_scalar(shi_s, S, -float(P // 2), 1.0 / P, ALU.add, ALU.mult))
            ln(v.tensor_scalar(shi_s, shi_s, ROUND, ROUND, ALU.add, ALU.subtract))
            ln(v.scalar_tensor_tensor(slo_s, shi_s, -float(P), S, ALU.mult, ALU.add))
            ln(v.tensor_scalar(U[0], raw[:, 4, :], dcol[:, 0:1], dcol[:, 1:2], ALU.mult, ALU.add))
            v.scalar_tensor_tensor(U[1], U[0], -1.0, U[0], ALU.mult, ALU.max)
        vector_block(edges1)
        with nc.Block() as block:
            @block.scalar
            def _(act):
                link(act, nc.scalar.activation(U[1], U[1], ACT.Exp, scale=-1.0), act_ch)
                nc.scalar.activation(U[2], U[1], ACT.Ln, bias=1.0)

        def edges2(v, ln):
            ln(v.scalar_tensor_tensor(U[2], U[0], 0.0, U[2], ALU.max, ALU.add))
            ln(v.tensor_tensor(base_s, U[2], raw[:, 3, :], ALU.mult))
            v.tensor_tensor(base_s, base_s, val_s, ALU.mult)
        vector_block(edges2)
        for part in (((S, src_idx), (Dst, dloc), (Ty, typed_idx), (shi_s, src_hi)), ((slo_s, src_lo), (base_s, base_w))):
            with nc.Block() as block:
                @block.tensor
                def _(pe):
                    for a, (s, d) in enumerate(part):
                        for g in range(8):
                            nc.tensor.transpose(ps[0:P, 2 * a + g // 4, (g % 4) * SG:(g % 4 + 1) * SG],
                                                s[:, g * P:(g + 1) * P], ident[0:SG, 0:SG])
            with nc.Block() as block:
                @block.vector
                def _(dve):
                    for a, (s, d) in enumerate(part):
                        nc.vector.tensor_copy(d[:, 0:T].rearrange("p (k n) -> p k n", k=2),
                                              ps[0:P, 2 * a:2 * a + 2, 0:4 * SG])

        def pad(v, ln):
            v.memset(src_idx[:, T:T + G], 0)
            v.memset(typed_idx[:, T:T + G], 0)
        vector_block(pad)

        def windows(g):
            return nc.values_load_multi_w_load_instructions(
                win_row[0:1, ds(g * G, G)], engines=(mybir.EngineType.DVE,), min_val=0, max_val=NW - 1,
                skip_runtime_bounds_check_because="bounded where the slots are laid out")[1]

        def after(g, least):
            return not isinstance(g, int) or g >= least

        def to_rows(v, out_ap, col, g, width=P):
            return v.tensor_tensor(out_ap, iota_row[:, 0:width].unsqueeze(1).to_broadcast([P, G, width]),
                                   bf(col[:, ds(g * G, G)], width), ALU.is_equal)

        def run(eng, step, lag):
            for g in range(4):
                step(g, g)
            with eng.Fori(1, NG // 4) as i:
                for k in range(4):
                    step(i * 4 + k, k)
            for g in range(NG, NG + lag):
                step(g, g % 4)

        def gather_engine(name, pool, table, idx, width, arrived, used):
            listed = sem(f"{name}_indices")

            nc.gpsimd.tensor_copy(group_idx[:, 0, :], idx[:, 0:G]).then_inc(listed, 1)

            def step(g, k):
                pool.wait_ge(listed, g + 1)
                if after(g, 3):
                    pool.wait_ge(used, g - 2)
                nc.gpsimd.tensor_copy(group_idx[:, (k + 1) % 4, :], idx[:, ds((g + 1) * G, G)]).then_inc(listed, 1)
                for j in range(G):
                    nc.gpsimd.indirect_dma_start(gath[:, k, :, :].rearrange("p j f -> p (j f)")[:, j * width:(j + 1) * width],
                                                 None, table,
                                                 bass.IndirectOffsetOnAxis(ap=group_idx[:, k, j:j + 1], axis=0)
                                                 ).then_inc(arrived[k], 16)
            run(pool, step, 0)

        def rows_of(k, width):
            return gath[:, k, :, :].rearrange("p j f -> p (j f)")[:, 0:G * width].rearrange("p (j f) -> p j f", f=width)

        def full(g, k):
            return (g - k) * (4 * G) + 16 * G

        def sum_pass(name, table, idx):
            arrived = [sem(f"{name}_rows{k}") for k in range(4)]
            hot = sem(f"{name}_onehot")
            summed = sem(f"{name}_slot_sums")
            added = sem(f"{name}_added")
            vector_block(lambda v, ln: v.memset(acc[:, 0:NW * D], 0.0))
            with nc.Block() as block:
                @block.gpsimd
                def _(pool):
                    gather_engine(name, pool, table, idx, D, arrived, summed)

                @block.tensor
                def _(pe):
                    def step(g, k):
                        pe.wait_ge(hot, g + 1)
                        pe.wait_ge(arrived[k], full(g, k))
                        if after(g, 2):
                            pe.wait_ge(added, (g - 1) * G)
                        for j in range(G):
                            last = nc.tensor.matmul(ps[0:P, k % 2, j * D:(j + 1) * D], onehot[:, k, j, :],
                                                    rows_of(k, D)[:, j, :], start=True, stop=True)
                        last.then_inc(summed, 1)
                    run(pe, step, 0)

                @block.vector
                def _(dve):
                    def step(g, k):
                        if not isinstance(g, int) or g < NG:
                            if after(g, 4):
                                dve.wait_ge(summed, g - 3)
                            to_rows(nc.vector, onehot[:, k, :, :], dloc, g).then_inc(hot, 1)
                        if after(g, 1):
                            w = windows(g - 1)
                            dve.wait_ge(summed, g)
                            for j in range(G):
                                if after(g, 2) or j:
                                    dve.wait_ge(added, (g - 1) * G + j)
                                a = acc[:, ds(w[j] * D, D)]
                                nc.vector.tensor_tensor(a, a, ps[0:P, (k + 1) % 2, j * D:(j + 1) * D], ALU.add
                                                        ).then_inc(added, 1)
                    run(dve, step, 1)

        def attention_pass(name, table, F, H, deg):
            MW = H * F + H + (1 if deg else 0)
            R = F + H
            arrived = [sem(f"{name}_rows{k}") for k in range(4)]
            hot, win_in, turned, hotT, dst_in_, terms = [sem(f"{name}_{n}") for n in
                ("onehot", "window_terms", "turned", "onehotT", "dst_terms", "chain")]
            logits, weighed, scaled, summed, added = [sem(f"{name}_{n}") for n in
                ("logits", "exp", "scaled_rows", "slot_sums", "added")]
            hotT_sb = arena[0:P, 9000:9000 + G * P].rearrange("p (j e) -> p j e", e=P)
            mov = [arena[0:P, b * G * MW:(b + 1) * G * MW].rearrange("p (j m) -> p j m", m=MW) for b in range(2)]
            sv = [slotv[:, i, 0:G * H].rearrange("p (j h) -> p j h", h=H) for i in range(10)]
            win_terms, s_sum, s_max, a_s, a_m = sv[0:5]
            arg, prob = sv[5:7], sv[7:9]
            dterm = ps[0:P, 6, 0:G * H].rearrange("p (j h) -> p j h", h=H)
            peak = alpha_max[:, 0:H].unsqueeze(1).to_broadcast([P, G, H])
            if deg:
                vector_block(lambda v, ln: [v.memset(m[:, :, MW - 1:MW], 1.0) for m in mov])
            with nc.Block() as block:
                @block.gpsimd
                def _(pool):
                    gather_engine(name, pool, table, src_idx, R, arrived, scaled)

                @block.scalar
                def _(act):
                    def step(g, k):
                        if not isinstance(g, int) or g < NG:
                            act.wait_ge(turned, g + 1)
                            if after(g, 1):
                                act.wait_ge(dst_in_, g)
                            nc.scalar.activation(hotT_sb.rearrange("p (b j) e -> p b (j e)", b=2), ps[0:P, 4:6, 0:4 * P],
                                                 ACT.Copy).then_inc(hotT, 1)
                        if after(g, 1):
                            b = (k + 3) % 4
                            q = b % 2
                            act.wait_ge(logits, g)
                            nc.scalar.activation(prob[q], arg[q], ACT.Exp).then_inc(weighed, 1)
                            act.wait_ge(weighed, g)
                            act.wait_ge(arrived[b], full(g - 1, b))
                            if after(g, 3):
                                act.wait_ge(summed, (g - 2) * G)
                            for j in range(G):
                                for a in range(H):
                                    nc.scalar.activation(mov[q][:, j, a * F:(a + 1) * F], rows_of(b, R)[:, j, 0:F],
                                                         ACT.Copy, scale=prob[q][:, j, a:a + 1])
                            nc.scalar.activation(mov[q][:, :, H * F:H * F + H], prob[q], ACT.Copy).then_inc(scaled, 1)
                    run(act, step, 1)

                @block.tensor
                def _(pe):
                    def step(g, k):
                        if not isinstance(g, int) or g < NG:
                            pe.wait_ge(hot, g + 1)
                            if after(g, 1):
                                pe.wait_ge(hotT, g)
                            for j in range(G):
                                last = nc.tensor.transpose(ps[0:P, 4 + j // 4, (j % 4) * P:(j % 4 + 1) * P],
                                                           onehot[:, k, j, :], ident[0:P, 0:P])
                            last.then_inc(turned, 1)
                            pe.wait_ge(hotT, g + 1)
                            pe.wait_ge(win_in, g + 1)
                            if after(g, 1):
                                pe.wait_ge(logits, g)
                            for j in range(G):
                                last = nc.tensor.matmul(dterm[:, j, :], hotT_sb[:, j, :], win_terms[:, j, :],
                                                        start=True, stop=True)
                            last.then_inc(dst_in_, 1)
                        if after(g, 2):
                            b = (k + 2) % 4
                            pe.wait_ge(scaled, g - 1)
                            for j in range(G):
                                if after(g, 3) or j > 1:
                                    pe.wait_ge(added, (g - 2) * G + j - 1)
                                lo = 0
                                for part in range(0, MW, 512 if MW <= 512 else 259):
                                    hi = min(MW, part + (512 if MW <= 512 else 259))
                                    last = nc.tensor.matmul(ps[0:P, 2 * (j % 2) + (part > 0), 0:hi - part],
                                                            onehot[:, b, j, :], mov[b % 2][:, j, part:hi], start=True, stop=True)
                                last.then_inc(summed, 1)
                    run(pe, step, 2)

                @block.vector
                def _(dve):
                    v = nc.vector

                    def step(g, k):
                        if not isinstance(g, int) or g < NG:
                            q = k % 2
                            if after(g, 4):
                                dve.wait_ge(summed, (g - 3) * G)
                            to_rows(v, onehot[:, k, :, :], dloc, g).then_inc(hot, 1)
                            w = windows(g)
                            if after(g, 1):
                                dve.wait_ge(dst_in_, g)
                            for j in range(G):
                                last = v.tensor_copy(win_terms[:, j, :], alpha_win[:, ds(w[j] * H, H)])
                            last.then_inc(win_in, 1)
                            dve.wait_ge(dst_in_, g + 1)
                            dve.wait_ge(arrived[k], full(g, k))
                            if after(g, 1):
                                dve.wait_ge(logits, g)
                            v.tensor_tensor(s_sum, dterm, rows_of(k, R)[:, :, F:R], ALU.add).then_inc(terms, 1)
                            v.tensor_tensor(a_s, dterm, peak, ALU.add).then_inc(terms, 1)
                            dve.wait_ge(terms, g * 4 + 2)
                            v.scalar_tensor_tensor(s_max, s_sum, SLOPE, s_sum, ALU.mult, ALU.max).then_inc(terms, 1)
                            v.scalar_tensor_tensor(a_m, a_s, SLOPE, a_s, ALU.mult, ALU.max).then_inc(terms, 1)
                            dve.wait_ge(terms, g * 4 + 4)
                            if after(g, 2):
                                dve.wait_ge(weighed, g - 1)
                            v.tensor_tensor(arg[q], s_max, a_m, ALU.subtract).then_inc(logits, 1)
                        if after(g, 2):
                            w = windows(g - 2)
                            for j in range(G):
                                dve.wait_ge(summed, (g - 2) * G + j + 1)
                                if after(g, 3) or j:
                                    dve.wait_ge(added, (g - 2) * G + j)
                                a = acc[:, ds(w[j] * MW, MW)]
                                if MW <= 512:
                                    v.tensor_tensor(a, a, ps[0:P, 2 * (j % 2), 0:MW], ALU.add).then_inc(added, 1)
                                else:
                                    v.tensor_tensor(acc[:, ds(w[j] * MW, 259)], acc[:, ds(w[j] * MW, 259)],
                                                    ps[0:P, 2 * (j % 2), 0:259], ALU.add)
                                    a = acc[:, ds(w[j] * MW + 259, MW - 259)]
                                    v.tensor_tensor(a, a, ps[0:P, 2 * (j % 2) + 1, 0:MW - 259], ALU.add).then_inc(added, 1)
                    run(dve, step, 2)

        def gat(name, X, F, H, CH, W, a_s, a_d, bias, out_ap, deg=False):
            MW = H * F + H + (1 if deg else 0)
            R = F + H
            HC = H * CH
            table = dram(f"{name}_table", [N, R])
            t1, t2 = tmp[0:F, 0:HC], tmp[0:F, 512:512 + HC]
            copies((wts[0:F, 0:HC], W), (t1, row(a_s.rearrange("h c -> (h c)"), F)),
                   (t2, row(a_d.rearrange("h c -> (h c)"), F)), (vecs[:, 0:CH], row(bias)))

            def att(v, ln):
                for k, t in enumerate((t1, t2)):
                    ln(v.tensor_tensor(t, t, wts[0:F, 0:HC], ALU.mult))
                    ln(v.tensor_reduce(watt[0:F, k * H:(k + 1) * H], t.rearrange("p (h c) -> p h c", c=CH), AX, ALU.add))
            vector_block(att)
            node_transpose([(lambda w: X[:, w, :], F, xT)])
            node_matmul([(window_of(xT, F), watt[0:F, 0:2 * H])], 2 * H,
                        lambda v, w, n: nc.vector.tensor_copy(alpha[:, w:w + n, 0:2 * H], v))

            def peak(v, ln):
                v.tensor_reduce(slotv[:, 15, 0:H], alpha[:, :, 0:H].rearrange("p w h -> p h w"), AX, ALU.max)
                v.tensor_copy(alpha_win[:, 0:NW * H].rearrange("p (w h) -> p w h", h=H), alpha[:, :, H:2 * H])
            vector_block(peak)
            tv = table.rearrange("(w p) f -> p w f", p=P)
            with nc.Block() as block:
                @block.sync
                def _(sp):
                    sp.dma_start(tv[:, :, 0:F], X).then_inc(dma.sem, 16)
                    sp.dma_start(tv[:, :, F:R], alpha[:, :, 0:H]).then_inc(dma.sem, 16)
                    dma.n += 32
                    sp.wait_ge(dma.sem, dma.n)

                @block.gpsimd
                def _(pool):
                    nc.gpsimd.partition_all_reduce(alpha_max[:, 0:H], slotv[:, 15, 0:H], P, RMAX)
            pr = [tmp[0:P, k * 100:k * 100 + NW * H].rearrange("p (w h) -> p w h", h=H) for k in range(4)]
            accv = acc[:, 0:NW * MW].rearrange("p (w m) -> p w m", m=MW)

            def self_terms(v, ln):
                ln(v.tensor_tensor(pr[0], alpha[:, :, 0:H], alpha[:, :, H:2 * H], ALU.add))
                ln(v.tensor_tensor(pr[1], alpha[:, :, H:2 * H], bw(alpha_max[:, 0:H]), ALU.add))
                ln(v.scalar_tensor_tensor(pr[2], pr[0], SLOPE, pr[0], ALU.mult, ALU.max))
                ln(v.scalar_tensor_tensor(pr[3], pr[1], SLOPE, pr[1], ALU.mult, ALU.max))
                v.tensor_tensor(pr[0], pr[2], pr[3], ALU.subtract)
            vector_block(self_terms)
            scalar_fn(pr[1], pr[0], ACT.Exp)

            def seed(v, ln):
                for a in range(H):
                    v.tensor_tensor(accv[:, :, a * F:(a + 1) * F], X, bf(pr[1][:, :, a], F), ALU.mult)
                v.tensor_copy(accv[:, :, H * F:H * F + H], pr[1])
                if deg:
                    v.memset(accv[:, :, MW - 1:MW], 0.0)
            vector_block(seed)
            attention_pass(name, table, F, H, deg)

            def divide(v, ln):
                ln(v.reciprocal(pr[0], accv[:, :, H * F:H * F + H]))
                for a in range(H):
                    c = accv[:, :, a * F:(a + 1) * F]
                    v.tensor_tensor(c, c, bf(pr[0][:, :, a], F), ALU.mult)
                if deg:
                    ln(v.tensor_scalar(inv_deg[:, :], accv[:, :, MW - 1], 1.0, None, ALU.max))
                    v.reciprocal(inv_deg[:, :], inv_deg[:, :])
            vector_block(divide)
            node_transpose([(lambda w, a=a: accv[:, w, a * F:(a + 1) * F], F, tT[a]) for a in range(H)])
            node_matmul([(window_of(tT[a], F), wts[0:F, a * CH:(a + 1) * CH]) for a in range(H)], CH,
                        lambda v, w, n: nc.vector.scalar_tensor_tensor(
                            out_ap[:, w:w + n, :], v, 1.0 / H,
                            vecs[:, 0:CH].unsqueeze(1).to_broadcast([P, n, CH]), ALU.mult, ALU.add))

        def norm_elu(gamma, beta):
            hsq = tmp[0:P, :].rearrange("p (w f) -> p w f", f=128)
            copies((vecs[:, 0:128], row(gamma)), (vecs[:, 128:256], row(beta)))
            column_sums(lambda w: h[:, w, :], stat[:, 0, :])

            def centre(v, ln):
                ln(v.tensor_scalar(stat[:, 0, :], stat[:, 0, :], 1.0 / N, None, ALU.mult))
                ln(v.tensor_tensor(h[:, :, :], h[:, :, :], bw(stat[:, 0, :]), ALU.subtract))
                v.tensor_tensor(hsq, h[:, :, :], h[:, :, :], ALU.mult)
            vector_block(centre)
            column_sums(lambda w: hsq[:, w, :], stat[:, 1, :])
            vector_block(lambda v, ln: v.tensor_scalar(stat[:, 1, :], stat[:, 1, :], 1.0 / N, BN_EPS, ALU.mult, ALU.add))
            scalar_fn(stat[:, 2, :], stat[:, 1, :], ACT.Sqrt)

            def scale(v, ln):
                ln(v.reciprocal(stat[:, 3, :], stat[:, 2, :]))
                ln(v.tensor_tensor(stat[:, 3, :], stat[:, 3, :], vecs[:, 0:128], ALU.mult))
                ln(v.tensor_tensor(h[:, :, :], h[:, :, :], bw(stat[:, 3, :]), ALU.mult))
                ln(v.tensor_tensor(h[:, :, :], h[:, :, :], bw(vecs[:, 128:256]), ALU.add))
                v.tensor_scalar(hsq, h[:, :, :], 0.0, None, ALU.min)
            vector_block(scale)
            scalar_fn(hsq, hsq, ACT.Exp)

            def elu(v, ln):
                ln(v.tensor_scalar(hsq, hsq, -1.0, None, ALU.add))
                v.scalar_tensor_tensor(h[:, :, :], h[:, :, :], 0.0, hsq, ALU.max, ALU.add)
            vector_block(elu)

        h64 = h[:, :, 0:D]

        gat("gat1", x[:, :, :], D, 4, 128, W1, as1, ad1, b1, h[:, :, :], deg=True)
        norm_elu(g1, be1)
        gat("gat2", h[:, :, :], 128, 4, 128, W2, as2, ad2, b2, h[:, :, :])
        norm_elu(g2, be2)
        gat("gat3", h[:, :, :], 128, 1, D, W3, as3, ad3, b3, h64)
        vector_block(lambda v, ln: v.tensor_tensor(x[:, :, :], x[:, :, :], h64, ALU.add))
        layernorm(x[:, :, :])

        cur = h[:, :, D:2 * D]
        vector_block(lambda v, ln: v.tensor_copy(cur[:, :, :], x[:, :, :]))
        accD = acc[:, 0:NW * D].rearrange("p (w f) -> p w f", f=D)
        for l in range(3):
            table = dram(f"sage{l}_table", [N, D])
            copies((table.rearrange("(w p) f -> p w f", p=P), cur[:, :, :]), (wts[0:D, 0:D], W_self[l]),
                   (wts[0:D, D:2 * D], W_neigh[l]), (vecs[:, 0:D], row(b_sage[l])))
            sum_pass(f"sage{l}", table, src_idx)
            vector_block(lambda v, ln: v.tensor_tensor(accD, accD, bf(inv_deg[:, :], D), ALU.mult))
            node_transpose([(lambda w: cur[:, w, :], D, tT[0]), (lambda w: accD[:, w, :], D, tT[1])])
            node_matmul([(window_of(tT[0], D), wts[0:D, 0:D]), (window_of(tT[1], D), wts[0:D, D:2 * D])], D,
                        lambda v, w, n: nc.vector.tensor_tensor(
                            cur[:, w:w + n, :], v, vecs[:, 0:D].unsqueeze(1).to_broadcast([P, n, D]), ALU.add))
            if l < 2:
                vector_block(lambda v, ln: v.tensor_scalar(cur[:, :, :], cur[:, :, :], 0.0, None, ALU.max))
        vector_block(lambda v, ln: v.tensor_tensor(x[:, :, :], x[:, :, :], cur[:, :, :], ALU.add))
        layernorm(x[:, :, :])

        typed = dram("typed_table", [N * NT, D])
        emn = tmp[:, 0:4 * D].rearrange("p (k h) -> p k h", h=D)
        ihn = tmp[0:96, 256:256 + 2 * D].rearrange("p (k h) -> p k h", h=D)
        hhn = tmp[0:96, 384:384 + 2 * D].rearrange("p (k h) -> p k h", h=D)
        emT = wts[0:D, 0:NT * D]
        gateT = tmp[0:D, 1024:1024 + 6 * D].rearrange("p (k g) -> p k g", k=2)
        copies((emn, edge_matrix.rearrange("t (m h) -> (t m) h", h=D).rearrange("(k p) h -> p k h", p=128)),
               (ihn, w_ih.rearrange("(k p) h -> p k h", p=96)), (hhn, w_hh.rearrange("(k p) h -> p k h", p=96)),
               (vecs[:, 0:3 * D], row(b_ih)), (vecs[:, 3 * D:6 * D], row(b_hh)))
        with nc.Block() as block:
            @block.tensor
            def _(pe):
                for k in range(4):
                    nc.tensor.transpose(ps[0:D, 0, k * 128:(k + 1) * 128], emn[:, k, :], ident[:, :])
                for k in range(2):
                    nc.tensor.transpose(ps[0:D, 1, k * 96:(k + 1) * 96], ihn[:, k, :], ident[0:96, 0:96])
                    nc.tensor.transpose(ps[0:D, 2, k * 96:(k + 1) * 96], hhn[:, k, :], ident[0:96, 0:96])

        def keep(v, ln):
            v.tensor_copy(emT, ps[0:D, 0, :])
            v.tensor_copy(gateT[:, 0, :], ps[0:D, 1, 0:3 * D])
            v.tensor_copy(gateT[:, 1, :], ps[0:D, 2, 0:3 * D])
        vector_block(keep)
        node_transpose([(lambda w: x[:, w, :], D, tT[0])])
        typed_sb = acc[:, 0:NW * NT * D].rearrange("p (w m) -> p w m", w=NW)
        node_matmul([(window_of(tT[0], D), emT)], NT * D,
                    lambda v, w, n: nc.vector.tensor_copy(typed_sb[:, w:w + n, :], v))
        copies((typed.rearrange("(w p t) f -> p w (t f)", p=P, t=NT), typed_sb))
        sum_pass("ggnn", typed, typed_idx)
        gates = arena[0:P, 2 * N:2 * N + NW * 192].rearrange("p (w g) -> p w g", g=192)
        node_transpose([(lambda w: x[:, w, :], D, tT[0]), (lambda w: accD[:, w, :], D, tT[1])])

        def biases(v, ln):
            v.tensor_tensor(vecs[:, 512:512 + 2 * D], vecs[:, 0:2 * D], vecs[:, 3 * D:5 * D], ALU.add)
            v.tensor_copy(vecs[:, 512 + 2 * D:512 + 3 * D], vecs[:, 2 * D:3 * D])
        vector_block(biases)
        node_matmul([(window_of(tT[1], D), gateT[:, 0, 0:2 * D]), (window_of(tT[0], D), gateT[:, 1, 0:2 * D])], 2 * D,
                    lambda v, w, n: nc.vector.tensor_tensor(
                        gates[:, w:w + n, 0:2 * D], v,
                        vecs[:, 512:512 + 2 * D].unsqueeze(1).to_broadcast([P, n, 2 * D]), ALU.add))
        node_matmul([(window_of(tT[1], D), gateT[:, 0, 2 * D:3 * D])], D,
                    lambda v, w, n: nc.vector.tensor_tensor(
                        gates[:, w:w + n, 2 * D:3 * D], v,
                        vecs[:, 2 * D:3 * D].unsqueeze(1).to_broadcast([P, n, D]), ALU.add))
        node_matmul([(window_of(tT[0], D), gateT[:, 1, 2 * D:3 * D])], D,
                    lambda v, w, n: nc.vector.tensor_tensor(
                        cur[:, w:w + n, :], v,
                        vecs[:, 5 * D:6 * D].unsqueeze(1).to_broadcast([P, n, D]), ALU.add))
        scalar_fn(gates[:, :, 0:2 * D], gates[:, :, 0:2 * D], ACT.Sigmoid)
        r_g, z_g, n_g = (gates[:, :, k * D:(k + 1) * D] for k in range(3))

        def fresh(v, ln):
            ln(v.tensor_tensor(cur[:, :, :], cur[:, :, :], r_g, ALU.mult))
            v.tensor_tensor(n_g, n_g, cur[:, :, :], ALU.add)
        vector_block(fresh)
        scalar_fn(n_g, n_g, ACT.Tanh)

        def blend(v, ln):
            ln(v.tensor_tensor(cur[:, :, :], x[:, :, :], n_g, ALU.subtract))
            ln(v.tensor_tensor(cur[:, :, :], cur[:, :, :], z_g, ALU.mult))
            ln(v.tensor_tensor(cur[:, :, :], cur[:, :, :], n_g, ALU.add))
            v.tensor_tensor(x[:, :, :], x[:, :, :], cur[:, :, :], ALU.add)
        vector_block(blend)
        layernorm(x[:, :, :])

        R3 = D + 1
        wh_table = dram("cos_table", [N, R3])
        wh = acc[:, 0:NW * R3].rearrange("p (w f) -> p w f", f=R3)
        pc = sb("pc", [P, 12])
        copies((wts[0:D, 0:D], W_cos), (vecs[:, 0:D], row(b_cos)), (pc[:, 0:3], row(coeff_param)),
               (pc[:, 3:4], row(scale_param)))
        node_transpose([(lambda w: x[:, w, :], D, tT[0])])
        node_matmul([(window_of(tT[0], D), wts[0:D, 0:D])], D,
                    lambda v, w, n: nc.vector.tensor_tensor(
                        wh[:, w:w + n, 0:D], v, vecs[:, 0:D].unsqueeze(1).to_broadcast([P, n, D]), ALU.add))
        sq3 = tmp[0:P, 0:NW * D].rearrange("p (w f) -> p w f", f=D)

        def norms(v, ln):
            ln(v.tensor_tensor(sq3, wh[:, :, 0:D], wh[:, :, 0:D], ALU.mult))
            v.tensor_reduce(small[:, 0, :], sq3, AX, ALU.add)
            ln(v.tensor_reduce(pc[:, 4:5], pc[:, 0:3], AX, ALU.max))
            ln(v.tensor_scalar(pc[:, 0:3], pc[:, 0:3], pc[:, 4:5], None, ALU.subtract))
            v.scalar_tensor_tensor(pc[:, 5:6], pc[:, 3:4], -1.0, pc[:, 3:4], ALU.mult, ALU.max)
        vector_block(norms)
        with nc.Block() as block:
            @block.scalar
            def _(act):
                nc.scalar.activation(wh[:, :, D], small[:, 0, :], ACT.Sqrt)
                nc.scalar.activation(pc[:, 8:11], pc[:, 0:3], ACT.Exp)
                link(act, nc.scalar.activation(pc[:, 6:7], pc[:, 5:6], ACT.Exp, scale=-1.0), act_ch)
                nc.scalar.activation(pc[:, 7:8], pc[:, 6:7], ACT.Ln, bias=1.0)

        def coeffs(v, ln):
            ln(v.tensor_reduce(pc[:, 4:5], pc[:, 8:11], AX, ALU.add))
            ln(v.reciprocal(pc[:, 5:6], pc[:, 4:5]))
            ln(v.tensor_scalar(pc[:, 8:11], pc[:, 8:11], pc[:, 5:6], None, ALU.mult))
            v.scalar_tensor_tensor(pc[:, 11:12], pc[:, 3:4], 0.0, pc[:, 7:8], ALU.max, ALU.add)
        vector_block(coeffs)
        c_pos, c_neg, c_own, c_scale = (pc[:, k:k + 1] for k in range(8, 12))
        copies((wh_table.rearrange("(w p) f -> p w f", p=P), wh))

        def cosine_pass():
            arrived = [sem(f"cos_rows{k}") for k in range(4)]
            hot, win_in, turned, hotT, dst_rows, hotlo = [sem(f"cos_{n}") for n in
                ("onehot", "window_rows", "turned", "onehotT", "dst_rows", "source_rows")]
            ch, weights, moved, done = [sem(f"cos_{n}") for n in ("chain", "weights", "products", "done")]
            hotT_sb = arena[0:P, 0:G * P].rearrange("p (j e) -> p j e", e=P)
            ring = [arena[0:P, 1000 + b * NW * D:1000 + (b + 1) * NW * D] for b in range(4)]
            win_rows = arena[0:P, 8000:8000 + G * R3].rearrange("p (j f) -> p j f", f=R3)
            wc = [arena[0:P, 9000 + b * 520:9000 + (b + 1) * 520] for b in range(2)]
            prod = arena[0:P, 10100:10100 + G * D].rearrange("p (j f) -> p j f", f=D)
            hi_w = [arena[0:P, 10700 + b * 200:10900 + b * 200].rearrange("p (j w) -> p j w", w=NW) for b in range(2)]
            hi_1 = arena[0:P, 11200:11400].rearrange("p (j w) -> p j w", w=NW)
            lo = [acc[:, 2000 + b * 1000:3000 + b * 1000].rearrange("p (j e) -> p j e", e=P) for b in range(2)]
            sv = [slotv[:, i, 0:G] for i in range(9)]
            dot, nn, rn, sim, tp, tn, tw, we = sv[0:8]
            zero = tmp[0:P, 0:400]
            vector_block(lambda v, ln: v.memset(zero, 0.0))
            flat = acc[:, 0:NW * R3]
            with nc.Block() as block:
                @block.gpsimd
                def _(pool):
                    gather_engine("cos", pool, wh_table, src_idx, R3, arrived, weights)

                @block.scalar
                def _(act):
                    def step(g, k):
                        act.wait_ge(turned, g + 1)
                        if after(g, 1):
                            act.wait_ge(dst_rows, g)
                        nc.scalar.activation(hotT_sb.rearrange("p (b j) e -> p b (j e)", b=2), ps[0:P, 4:6, 0:4 * P],
                                             ACT.Copy).then_inc(hotT, 1)
                    run(act, step, 0)

                @block.tensor
                def _(pe):
                    for c in range(4):
                        nc.tensor.matmul(ps[0:P, c, 0:400], ones[:, :], zero, start=True, stop=False)

                    def step(g, k):
                        if not isinstance(g, int) or g < NG:
                            pe.wait_ge(hot, g + 1)
                            if after(g, 1):
                                pe.wait_ge(hotT, g)
                            for j in range(G):
                                last = nc.tensor.transpose(ps[0:P, 4 + j // 4, (j % 4) * P:(j % 4 + 1) * P],
                                                           onehot[:, k, j, :], ident[0:P, 0:P])
                            last.then_inc(turned, 1)
                            pe.wait_ge(hotT, g + 1)
                            pe.wait_ge(win_in, g + 1)
                            if after(g, 1):
                                pe.wait_ge(weights, g)
                            for j in range(G):
                                last = nc.tensor.matmul(ps[0:P, 6 + j // 4, (j % 4) * R3:(j % 4 + 1) * R3],
                                                        hotT_sb[:, j, :], win_rows[:, j, :], start=True, stop=True)
                            last.then_inc(dst_rows, 1)
                        if after(g, 1):
                            for j in range(G):
                                pe.wait_ge(moved, (g - 1) * G + j + 1)
                                for c in range(4):
                                    last = nc.tensor.matmul(ps[0:P, c, 0:400], lo[(k + 1) % 2][:, j, :],
                                                            ring[j % 4][:, c * 400:(c + 1) * 400], start=False, stop=False)
                                last.then_inc(done, 1)
                    run(pe, step, 1)
                    for c in range(4):
                        nc.tensor.matmul(ps[0:P, c, 0:400], ones[:, :], zero, start=False, stop=True)

                @block.vector
                def _(dve):
                    v = nc.vector

                    def step(g, k):
                        q = k % 2
                        if not isinstance(g, int) or g < NG:
                            if after(g, 4):
                                dve.wait_ge(turned, g - 3)
                            to_rows(v, onehot[:, k, :, :], dloc, g).then_inc(hot, 1)
                            w = windows(g)
                            if after(g, 1):
                                dve.wait_ge(dst_rows, g)
                            for j in range(G):
                                last = v.tensor_copy(win_rows[:, j, :], flat[:, ds(w[j] * R3, R3)])
                            last.then_inc(win_in, 1)
                            if after(g, 2):
                                dve.wait_ge(done, (g - 1) * G)
                            to_rows(v, lo[q], src_lo, g)
                            dve.wait_ge(dst_rows, g + 1)
                            dve.wait_ge(arrived[k], full(g, k))
                            n = [g * 11]

                            def ln(ins, wait=True):
                                n[0] = n[0] + 1
                                ins.then_inc(ch, 1)
                                if wait:
                                    dve.wait_ge(ch, n[0])
                            wcq = wc[q].rearrange("p (j f) -> p j f", f=R3)
                            gk = rows_of(k, R3)
                            ln(to_rows(v, hi_1, src_hi, g, NW), wait=False)
                            ln(v.tensor_copy(wc[q].rearrange("p (b m) -> p b m", b=2), ps[0:P, 6:8, 0:4 * R3]))
                            ln(v.tensor_tensor(prod, gk[:, :, 0:D], wcq[:, :, 0:D], ALU.mult))
                            ln(v.tensor_tensor(nn, gk[:, :, D], wcq[:, :, D], ALU.mult))
                            ln(v.tensor_scalar(nn, nn, SIM_EPS, None, ALU.max))
                            ln(v.reciprocal(rn, nn), wait=False)
                            ln(v.tensor_reduce(dot, prod, AX, ALU.add))
                            ln(v.tensor_tensor(sim, dot, rn, ALU.mult))
                            ln(v.tensor_scalar(tp, sim, 0.0, c_pos, ALU.max, ALU.mult), wait=False)
                            ln(v.tensor_scalar(tn, sim, 0.0, c_neg, ALU.min, ALU.mult))
                            ln(v.tensor_tensor(tw, tp, tn, ALU.add))
                            v.tensor_tensor(we, tw, base_w[:, ds(g * G, G)], ALU.mult).then_inc(weights, 1)
                            dve.wait_ge(weights, g + 1)
                            v.tensor_tensor(hi_w[q], hi_1, bf(we, NW), ALU.mult).then_inc(hotlo, 1)
                        if after(g, 1):
                            dve.wait_ge(hotlo, g)
                            p = (k + 1) % 2
                            wcp = wc[p].rearrange("p (j f) -> p j f", f=R3)
                            for j in range(G):
                                if after(g, 2) or j >= 4:
                                    dve.wait_ge(done, (g - 1) * G + j - 3)
                                v.tensor_tensor(ring[j % 4].rearrange("p (w f) -> p w f", f=D), bf(hi_w[p][:, j, :], D),
                                                wcp[:, j, 0:D].unsqueeze(1).to_broadcast([P, NW, D]), ALU.mult
                                                ).then_inc(moved, 1)
                    run(dve, step, 1)

        cosine_pass()

        def gathered(v, ln):
            t3 = tmp[0:P, 0:NW * D].rearrange("p (w f) -> p w f", f=D)
            ln(v.tensor_scalar(t3, wh[:, :, 0:D], c_own, None, ALU.mult))
            ln(v.tensor_tensor(t3.rearrange("p w f -> p (w f)").rearrange("p (c n) -> p c n", c=4),
                               t3.rearrange("p w f -> p (w f)").rearrange("p (c n) -> p c n", c=4), ps[0:P, 0:4, 0:400], ALU.add))
            v.scalar_tensor_tensor(x[:, :, :], t3, c_scale, x[:, :, :], ALU.mult, ALU.add)
        vector_block(gathered)
        layernorm(x[:, :, :])
        copies((out.rearrange("(w p) f -> p w f", p=P), x[:, :, :]))


_INS = ['x', 'src', 'dst', 'edge_type_8', 'edge_weight', 'edge_weight_n2',
        'L0_gnn_W1', 'L0_gnn_as1', 'L0_gnn_ad1', 'L0_gnn_b1', 'L0_gnn_g1', 'L0_gnn_be1',
        'L0_gnn_W2', 'L0_gnn_as2', 'L0_gnn_ad2', 'L0_gnn_b2', 'L0_gnn_g2', 'L0_gnn_be2',
        'L0_gnn_W3', 'L0_gnn_as3', 'L0_gnn_ad3', 'L0_gnn_b3',
        'L1_gnn_W_self', 'L1_gnn_W_neigh', 'L1_gnn_b',
        'L2_gnn_edge_matrix', 'L2_gnn_w_ih', 'L2_gnn_w_hh', 'L2_gnn_b_ih', 'L2_gnn_b_hh',
        'L3_gnn_W', 'L3_gnn_b', 'L3_gnn_deg_coeff', 'L3_gnn_coeff_param', 'L3_gnn_scale_param']
_OUTS = [((N, D), 'float32')]


def kernel(**inputs):
    import numpy as _np
    import concourse.bacc as _bacc
    from concourse import mybir as _mybir
    from concourse.bass_utils import run_bass_kernel_spmd as _run

    nc = _bacc.Bacc("TRN2", target_bir_lowering=False, num_devices=1)
    arrays, args = {}, []
    for name in _INS:
        a = _np.ascontiguousarray(inputs[name])
        arrays[f"in_{name}_dram"] = a
        args.append(nc.dram_tensor(f"in_{name}_dram", a.shape, _mybir.dt.from_np(a.dtype), kind="ExternalInput").ap())
    for i, (shape, dtype) in enumerate(_OUTS):
        dt = _mybir.dt.from_np(_np.dtype(dtype))
        args.append(nc.dram_tensor(f"out_{i}_dram", shape, dt, kind="ExternalOutput").ap())
    gnn_kernel(nc, *args)
    r = _run(nc, [arrays], core_ids=[0])
    return r.results[0]["out_0_dram"]
```

```python
import numpy as np
import concourse.bass as bass
from concourse import mybir
from concourse.alu_op_type import AluOpType as ALU

ACT = mybir.ActivationFunctionType
AX = mybir.AxisListType.X
F32 = mybir.dt.float32
I32 = mybir.dt.int32
I16 = mybir.dt.int16
BF16 = mybir.dt.bfloat16
RMAX = bass.bass_isa.ReduceOp.max
ds = bass.ds

P = 125
N = 3125
NW = N // P
E = 100000
C = E // P
G = 8
T = 832
NG = T // G
SG = T // 8
D = 64
NT = 8
WG = 3
PT = 5
ROUND = 12582912.0
LN_EPS = 1e-5
BN_EPS = 1e-5
SIM_EPS = 1e-8
SLOPE = 0.2


class Counted:

    def __init__(self, nc, ctx, name):
        self.sem = ctx.enter_context(nc.semaphore(name))
        self.n = 0


def gnn_kernel(nc, x_in, src_in, dst_in, type_in, w1_in, w2_in,
               W1, as1, ad1, b1, g1, be1, W2, as2, ad2, b2, g2, be2, W3, as3, ad3, b3,
               W_self, W_neigh, b_sage, edge_matrix, w_ih, w_hh, b_ih, b_hh,
               W_cos, b_cos, deg_coeff, coeff_param, scale_param, out):
    from contextlib import ExitStack
    ctx = ExitStack()
    with ctx:
        ctx.enter_context(nc.allow_non_contiguous_dma(reason="one column of small tables"))

        def sb(name, shape, dt=F32):
            return ctx.enter_context(nc.sbuf_tensor(name, shape, dt))

        def dram(name, shape, dt=F32):
            return nc.dram_tensor(name, shape, dt, kind="Internal").ap()

        def sem(name):
            return ctx.enter_context(nc.semaphore(name))

        dloc = sb("dloc", [P, T])
        sloc = sb("sloc", [P, T])
        base_w = sb("base_w", [P, T])
        cos_idx = sb("cos_idx", [P, T + G], I32)
        typed_idx = sb("typed_idx", [P, T + G], I32)
        win_row = sb("win_row", [1, T], I32)
        cos_win_row = sb("cos_win_row", [1, T], I32)
        acc = sb("acc", [P, NW * 517])
        arena = sb("arena", [128, 12912])
        stage = sb("stage", [P, PT * WG * PT * P])
        gath = stage[:, 0:4 * G * 132].rearrange("p (k j f) -> p k j f", k=4, j=G)
        onehot = stage[:, 4224:4224 + 4 * G * P].rearrange("p (k j f) -> p k j f", k=4, j=G)
        pieces = [stage[:, q * WG * PT * P:(q + 1) * WG * PT * P].rearrange("p (w b d) -> p w b d", w=WG, b=PT)
                  for q in range(PT)]
        group_idx = sb("group_idx", [P, 4, G], I32)
        x = sb("x", [P, NW, D])
        h = sb("h", [P, NW, 128])
        hflat = h[:, :, :].rearrange("p w f -> p (w f)")
        minus_one = sb("minus_one", [P, 1])
        tmp = sb("tmp", [128, NW * 128])
        iota_row = sb("iota_row", [P, P])
        ident = sb("ident", [128, 128])
        ones = sb("ones", [P, P])
        alpha = sb("alpha", [P, NW, 8])
        alpha_max = sb("alpha_max", [P, 4])
        inv_deg = sb("inv_deg", [P, NW])
        wts = sb("wts", [128, 512])
        watt = sb("watt", [128, 8])
        vecs = sb("vecs", [P, 1024])
        stat = sb("stat", [P, 4, 128])
        small = sb("small", [P, 8, NW])
        slotv = sb("slotv", [P, 16, G * 4])
        ps = ctx.enter_context(nc.psum_tensor("ps", [128, 8, 512], F32))

        xT = arena[:, 0:N]
        tT = [arena[:, i * N:(i + 1) * N] for i in range(4)]

        dma = Counted(nc, ctx, "dma_done")
        chain = Counted(nc, ctx, "vector_chain")
        node_mm = Counted(nc, ctx, "node_products_ready")
        node_ev = Counted(nc, ctx, "node_products_read")
        act_ch = Counted(nc, ctx, "scalar_chain")
        pool_ch = Counted(nc, ctx, "pool_chain")

        def link(eng, ins, counted=chain):
            counted.n += 1
            ins.then_inc(counted.sem, 1)
            eng.wait_ge(counted.sem, counted.n)

        def copies(*pairs):
            with nc.Block() as block:
                @block.sync
                def _(sp):
                    for dst_ap, src_ap in pairs:
                        sp.dma_start(dst_ap, src_ap).then_inc(dma.sem, 16)
                        dma.n += 16
                    sp.wait_ge(dma.sem, dma.n)

        def row(ap, parts=P):
            return ap.unsqueeze(0).to_broadcast([parts, ap.shape[0]])

        def bw(ap, width=None):
            return ap.unsqueeze(1).to_broadcast([ap.shape[0], NW, ap.shape[-1]])

        def bf(ap, n):
            return ap.unsqueeze(len(ap.shape)).to_broadcast([*ap.shape, n])

        def scalar_fn(out_ap, in_ap, fn, **kw):
            with nc.Block() as block:
                @block.scalar
                def _(act):
                    nc.scalar.activation(out_ap, in_ap, fn, **kw)

        def vector_block(body):
            with nc.Block() as block:
                @block.vector
                def _(dve):
                    body(nc.vector, lambda ins: link(dve, ins))

        def node_transpose(jobs):
            rounds = [(s, f, d, w) for s, f, d in jobs for w in range(0, NW, 4)]
            m0, e0 = node_mm.n, node_ev.n
            with nc.Block() as block:
                @block.tensor
                def _(pe):
                    for r, (s, f, d, w0) in enumerate(rounds):
                        if r >= 8:
                            pe.wait_ge(node_ev.sem, e0 + r - 7)
                        for k, w in enumerate(range(w0, min(w0 + 4, NW))):
                            last = nc.tensor.transpose(ps[0:f, r % 8, k * P:(k + 1) * P], s(w), ident[0:P, 0:P])
                        last.then_inc(node_mm.sem, 1)

                @block.vector
                def _(dve):
                    for r, (s, f, d, w0) in enumerate(rounds):
                        n = (min(w0 + 4, NW) - w0) * P
                        dve.wait_ge(node_mm.sem, m0 + r + 1)
                        nc.vector.tensor_copy(d[0:f, w0 * P:w0 * P + n], ps[0:f, r % 8, 0:n]).then_inc(node_ev.sem, 1)
            node_mm.n += len(rounds)
            node_ev.n += len(rounds)

        def node_matmul(terms, width, read):
            per = min(4, 512 // width)
            rounds = list(range(0, NW, per))
            m0, e0 = node_mm.n, node_ev.n
            with nc.Block() as block:
                @block.tensor
                def _(pe):
                    for r, w0 in enumerate(rounds):
                        if r >= 8:
                            pe.wait_ge(node_ev.sem, e0 + r - 7)
                        for k, w in enumerate(range(w0, min(w0 + per, NW))):
                            for i, (lhsT, rhs) in enumerate(terms):
                                last = nc.tensor.matmul(ps[0:P, r % 8, k * width:(k + 1) * width], lhsT(w), rhs,
                                                        start=(i == 0), stop=(i == len(terms) - 1))
                        last.then_inc(node_mm.sem, 1)

                @block.vector
                def _(dve):
                    for r, w0 in enumerate(rounds):
                        n = min(w0 + per, NW) - w0
                        dve.wait_ge(node_mm.sem, m0 + r + 1)
                        v = ps[0:P, r % 8, 0:n * width].rearrange("p (k c) -> p k c", c=width)
                        read(v, w0, n).then_inc(node_ev.sem, 1)
            node_mm.n += len(rounds)
            node_ev.n += len(rounds)

        def window_of(t, f):
            return lambda w: t[0:f, w * P:(w + 1) * P]

        def column_sums(table, out_ap):
            m0 = node_mm.n
            with nc.Block() as block:
                @block.tensor
                def _(pe):
                    for w in range(NW):
                        last = nc.tensor.matmul(ps[0:P, 0, 0:128], ones[:, :], table(w), start=(w == 0), stop=(w == NW - 1))
                    last.then_inc(node_mm.sem, 1)

                @block.vector
                def _(dve):
                    dve.wait_ge(node_mm.sem, m0 + 1)
                    nc.vector.tensor_copy(out_ap, ps[0:P, 0, 0:128])
            node_mm.n += 1

        def layernorm(t):
            sq = tmp[0:P, 0:NW * D].rearrange("p (w f) -> p w f", f=D)

            def centre(v, ln):
                ln(v.tensor_reduce(small[:, 0, :], t, AX, ALU.add))
                ln(v.tensor_scalar(small[:, 0, :], small[:, 0, :], 1.0 / D, None, ALU.mult))
                ln(v.tensor_tensor(t, t, bf(small[:, 0, :], D), ALU.subtract))
                ln(v.tensor_tensor(sq, t, t, ALU.mult))
                ln(v.tensor_reduce(small[:, 1, :], sq, AX, ALU.add))
                v.tensor_scalar(small[:, 1, :], small[:, 1, :], 1.0 / D, LN_EPS, ALU.mult, ALU.add)
            vector_block(centre)
            scalar_fn(small[:, 2, :], small[:, 1, :], ACT.Sqrt)

            def scale(v, ln):
                ln(v.reciprocal(small[:, 3, :], small[:, 2, :]))
                v.tensor_tensor(t, t, bf(small[:, 3, :], D), ALU.mult)
            vector_block(scale)

        def after(g, least):
            return not isinstance(g, int) or g >= least

        def run(eng, step, lag, groups=NG):
            for g in range(4):
                step(g, g)
            with eng.Fori(1, groups // 4) as i:
                for k in range(4):
                    step(i * 4 + k, k)
            for g in range(groups, groups + lag):
                step(g, g % 4)

        def full(g, k):
            return (g - k) * (4 * G) + 16 * G

        ciota = hflat[0:1, 0:C].bitcast(I32)
        tcol = sb("tcol", [SG, 8], I32)
        slot_c = sb("slot_c", [SG, 8])
        slot_w = sb("slot_w", [SG, 8])
        slot_t = sb("slot_t", [SG, 8])
        slot_ci = sb("slot_ci", [SG, 8], I32)
        slot_wi = sb("slot_wi", [SG, 8], I32)
        iota_i = arena[0:P, 0:P].bitcast(I32)
        dcol = sb("dcol", [SG, 2])
        before = hflat[:, 1000:1000 + P]
        disorder = sb("disorder", [P, 4])
        flag = sb("flag", [P, 1], I32)

        edge_tab = [dram(n, [E], t) for n, t in (("src_list", I32), ("dst_list", I32), ("type_list", I32),
                                                 ("w1_list", F32), ("w2_list", F32))]
        edge_in = (src_in, dst_in, type_in, w1_in, w2_in)
        QP = 123
        this_d = acc[0:QP, 0:(E - 1) // QP].bitcast(I32)
        next_d = acc[0:QP, 1000:1000 + (E - 1) // QP].bitcast(I32)
        copies(*[(t, i) for t, i in zip(edge_tab, edge_in)],
               (this_d, dst_in[0:E - 1].rearrange("(p n) -> p n", p=QP)),
               (next_d, dst_in[1:E].rearrange("(p n) -> p n", p=QP)),
               (x[:, :, :], x_in.rearrange("(w p) f -> p w f", p=P)),
               (dcol[:, :], row(deg_coeff, SG)))
        with nc.Block() as block:
            @block.gpsimd
            def _(pool):
                nc.gpsimd.iota(iota_i, [[1, P]], base=0, channel_multiplier=0)
                nc.gpsimd.iota(ciota[:, :], [[1, C]], base=0, channel_multiplier=0)
                nc.gpsimd.iota(tcol[:, :], [[SG, 8]], base=0, channel_multiplier=1)
                nc.gpsimd.memset(before[:, :], 1.0)
                link(pool, nc.gpsimd.memset(ident[:, :], 0.0), pool_ch)
                nc.gpsimd.affine_select(out=ident[:, :], in_=ident[:, :], compare_op=ALU.not_equal, fill=1.0,
                                        base=0, pattern=[[-1, 128]], channel_multiplier=1)
                nc.gpsimd.affine_select(out=before[:, :], in_=before[:, :], compare_op=ALU.is_gt, fill=0.0,
                                        base=0, pattern=[[1, P]], channel_multiplier=-1)
                nc.gpsimd.memset(ones[:, :], 1.0)

        def in_order(v, ln):
            v.tensor_copy(iota_row[:, :], iota_i)
            v.tensor_copy(slot_t[:, :], tcol[:, :])
            v.memset(minus_one[:, :], -1.0)
            d = acc[0:QP, 2000:2000 + (E - 1) // QP]
            ln(v.memset(disorder[:, :], 0.0))
            ln(v.tensor_tensor(d, this_d, next_d, ALU.is_gt))
            v.tensor_reduce(disorder[0:QP, 0:1], d, AX, ALU.max)
        vector_block(in_order)
        with nc.Block() as block:
            @block.gpsimd
            def _(pool):
                nc.gpsimd.partition_all_reduce(disorder[:, 1:2], disorder[:, 0:1], P, RMAX)
        vector_block(lambda v, ln: v.tensor_copy(flag[:, :], disorder[:, 1:2]))

        def when(eng, cond, body):
            if cond is None:
                body()
                return
            value = eng.value_load(cond, min_val=0, max_val=1)
            with eng.If(value > 0):
                body()
            with eng.Else():
                eng.nop()

        REC = arena[0:P, 0:5 * (C + G)]
        pos = arena[0:P, 4200:4200 + T + G].bitcast(I32)
        key = arena[0:P, 5100:5100 + T]

        def bucket(name, n, K, rec, nf, table, cond, beside=None):
            per = {832: 13, 800: 10}[n]
            cb, nb = 8 * per, n // (8 * per)
            w = K * cb
            oh, tot, scan, fresh = (acc[:, i * w:(i + 1) * w] for i in range(4))
            kc = lambda t: t.rearrange("p (k c) -> p k c", c=cb)
            pieces = lambda t: t.rearrange("p (b m) -> p b m", b=8)
            banks = ps[0:P, 0:8, 0:K * per]
            part, hist, incl, carry, step_sum = (slotv[:, i, 0:K] for i in range(5))
            steps = sem(f"{name}_chain")
            hot, totals, kept, ranks, used, placed = [sem(f"{name}_{s}") for s in
                ("onehot", "totals", "totals_kept", "ranks", "ranks_used", "positions")]
            counted = sem(f"{name}_histogram")
            listed = sem(f"{name}_listed")
            landed = [sem(f"{name}_landed{k}") for k in range(4)]
            recv = rec[:, 0:(n + G) * nf]
            with nc.Block() as block:
                @block.vector
                def _(dve):
                    v = nc.vector
                    m = [0]

                    def ln(ins):
                        m[0] += 1
                        ins.then_inc(steps, 1)
                        dve.wait_ge(steps, m[0])

                    def onehot(b):
                        return v.tensor_tensor(kc(oh), iota_row[:, 0:K].unsqueeze(2).to_broadcast([P, K, cb]),
                                               key[:, b * cb:(b + 1) * cb].unsqueeze(1).to_broadcast([P, K, cb]),
                                               ALU.is_equal)

                    def body():
                        v.memset(pos[:, n:n + G], 0)
                        v.memset(recv[:, n * nf:(n + G) * nf], 0.0)
                        ln(v.memset(fresh, 1.0))
                        ln(v.memset(kc(fresh)[:, :, 0:1], 0.0))
                        ln(v.memset(hist, 0.0))
                        for b in range(nb):
                            ln(onehot(b))
                            ln(v.tensor_reduce(part, kc(oh), AX, ALU.add))
                            ln(v.tensor_tensor(hist, hist, part, ALU.add))
                        v.tensor_copy(incl, hist).then_inc(counted, 1)
                        dve.wait_ge(totals, 1)
                        ln(v.tensor_copy(hist, ps[0:P, 0, 0:K]))
                        ln(v.tensor_tensor_scan(incl, ones[:, 0:K], hist, 0.0, ALU.mult, ALU.add))
                        ln(v.tensor_tensor(carry, incl, hist, ALU.subtract))
                        for b in range(nb):
                            onehot(b).then_inc(hot, 1)
                            dve.wait_ge(totals, b + 2)
                            v.tensor_copy(pieces(tot), banks).then_inc(kept, 1)
                            dve.wait_ge(kept, b + 1)
                            ln(v.tensor_tensor_scan(scan, fresh, tot, 0.0, ALU.mult, ALU.add))
                            ln(v.tensor_tensor(scan, scan, tot, ALU.subtract))
                            ln(v.tensor_reduce(step_sum, kc(tot), AX, ALU.add))
                            dve.wait_ge(ranks, b + 1)
                            v.tensor_tensor(pieces(scan), pieces(scan), banks, ALU.add).then_inc(used, 1)
                            dve.wait_ge(used, b + 1)
                            ln(v.tensor_tensor(kc(scan), kc(scan), bf(carry, cb), ALU.add))
                            ln(v.tensor_tensor(scan, scan, oh, ALU.mult))
                            ln(v.tensor_tensor(carry, carry, step_sum, ALU.add))
                            v.tensor_reduce(tot[:, 0:cb], scan.rearrange("p (k c) -> p c k", c=cb), AX, ALU.add
                                            ).then_inc(steps, 1)
                            m[0] += 1
                            dve.wait_ge(steps, m[0])
                            v.tensor_copy(pos[:, b * cb:(b + 1) * cb], tot[:, 0:cb]).then_inc(placed, 1)
                            dve.wait_ge(placed, b + 1)
                    when(dve, cond, body)
                    if beside:
                        beside["vector"](dve)

                @block.tensor
                def _(pe):
                    def products(lhsT, done):
                        for j in range(8):
                            last = nc.tensor.matmul(ps[0:P, j, 0:K * per], lhsT, oh[:, j * K * per:(j + 1) * K * per],
                                                    start=True, stop=True)
                        last.then_inc(done, 1)

                    def body():
                        pe.wait_ge(counted, 1)
                        nc.tensor.matmul(ps[0:P, 0, 0:K], ones[:, :], incl, start=True, stop=True).then_inc(totals, 1)
                        for b in range(nb):
                            pe.wait_ge(hot, b + 1)
                            products(ones[:, :], totals)
                            pe.wait_ge(kept, b + 1)
                            products(before[:, :], ranks)
                    when(pe, cond, body)
                    if beside:
                        pe.wait_ge(used, nb)
                        beside["tensor"](pe)

                if beside:
                    @block.scalar
                    def _(act):
                        beside["scalar"](act)

                    @block.sync
                    def _(sp):
                        beside["sync"](sp)

                @block.gpsimd
                def _(pool):
                    def body():
                        def list_group(g, k):
                            nc.gpsimd.tensor_copy(group_idx[:, k, :], pos[:, ds(g * G, G)])
                            nc.gpsimd.tensor_copy(rows_of(k, nf), recv[:, ds(g * (G * nf), G * nf)].rearrange(
                                "p (j f) -> p j f", f=nf)).then_inc(listed, 1)
                        pool.wait_ge(placed, nb)
                        list_group(0, 0)

                        def step(g, k):
                            pool.wait_ge(listed, g + 1)
                            if after(g, 3):
                                pool.wait_ge(landed[(k + 1) % 4], full(g - 3, (k + 1) % 4))
                            list_group(g + 1, (k + 1) % 4)
                            for j in range(G):
                                nc.gpsimd.indirect_dma_start(
                                    table, bass.IndirectOffsetOnAxis(ap=group_idx[:, k, j:j + 1], axis=0),
                                    rows_of(k, nf)[:, j, :], None).then_inc(landed[k], 16)
                        run(pool, step, 0, n // G)
                        for k in range(4):
                            pool.wait_ge(landed[k], n // 4 * 16)
                    when(pool, cond, body)

        CH = 100
        listv = acc[0:CH, 0:5 * 1000].rearrange("p (a g e) -> p a g e", a=5, e=P)
        listf = [acc[0:CH, 5000 + a * 1000:6000 + a * 1000] for a in range(3)]
        fb_dma, fb_f, fb_t, fb_e = [sem(f"lists_{n}") for n in ("loaded", "as_float", "turned", "read")]
        fb_ch = sem("lists_chain")
        rec5 = REC[:, 0:C * 5].rearrange("p (c f) -> p c f", f=5)
        with nc.Block() as block:
            @block.sync
            def _(sp):
                def body():
                    for a, t in enumerate(edge_in):
                        o = listv[:, a, :, :]
                        sp.dma_start(o if a > 2 else o.bitcast(I32),
                                     t.rearrange("(g p e) -> p g e", p=CH, e=P)).then_inc(fb_dma, 16)
                    sp.wait_ge(fb_dma, 5 * 16)
                when(sp, flag[0:1, 0:1], body)

            @block.tensor
            def _(pe):
                def body():
                    pe.wait_ge(fb_f, 3)
                    for a in range(5):
                        s = listf[a].rearrange("p (g e) -> p g e", e=P) if a < 3 else listv[:, a, :, :]
                        if a >= 4:
                            pe.wait_ge(fb_e, a - 3)
                        for g in range(8):
                            last = nc.tensor.transpose(ps[0:P, 2 * (a % 4) + g // 4, (g % 4) * CH:(g % 4 + 1) * CH],
                                                       s[:, g, :], ident[0:CH, 0:CH])
                        last.then_inc(fb_t, 1)
                when(pe, flag[0:1, 0:1], body)

            @block.vector
            def _(dve):
                v = nc.vector

                def body():
                    dve.wait_ge(fb_dma, 5 * 16)
                    for a in range(3):
                        v.tensor_copy(listf[a].rearrange("p (g e) -> p g e", e=P),
                                      listv[:, a, :, :].bitcast(I32)).then_inc(fb_f, 1)
                    for a in range(5):
                        dve.wait_ge(fb_t, a + 1)
                        banks = ps[0:P, 2 * (a % 4):2 * (a % 4) + 2, 0:4 * CH]
                        if a == 1:
                            v.tensor_copy(key[:, 0:C].rearrange("p (b n) -> p b n", b=2), banks).then_inc(fb_ch, 1)
                        o = rec5[:, :, a] if a > 2 else rec5[:, :, a].bitcast(I32)
                        v.tensor_copy(o.rearrange("p (b n) -> p b n", b=2), banks).then_inc(fb_e, 1)
                    dve.wait_ge(fb_ch, 1)
                    v.tensor_scalar(key[:, 0:C], key[:, 0:C], -float(P // 2), 1.0 / P, ALU.add, ALU.mult).then_inc(fb_ch, 1)
                    dve.wait_ge(fb_ch, 2)
                    v.tensor_scalar(key[:, 0:C], key[:, 0:C], ROUND, ROUND, ALU.add, ALU.subtract).then_inc(fb_ch, 1)
                    dve.wait_ge(fb_ch, 3)
                when(dve, flag[0:1, 0:1], body)
        order_tab = dram("order_table", [E, 5])

        def rows_of(k, width):
            return gath[:, k, :, :].rearrange("p j f -> p (j f)")[:, 0:G * width].rearrange("p (j f) -> p j f", f=width)

        bucket("order", C, NW, REC, 5, order_tab, flag[0:1, 0:1])
        lists_out = sem("lists_out")
        with nc.Block() as block:
            @block.sync
            def _(sp):
                def body():
                    for a, t in enumerate(edge_tab):
                        s = order_tab[:, a:a + 1].rearrange("n f -> (n f)")
                        sp.dma_start(t, s if a > 2 else s.bitcast(I32)).then_inc(lists_out, 16)
                    sp.wait_ge(lists_out, 5 * 16)
                when(sp, flag[0:1, 0:1], body)

        lastd = tmp[0:1, 0:C]
        lastw = tmp[0:1, C:2 * C]
        U = [tmp[0:SG, k * 1000:(k + 1) * 1000] for k in range(3)]

        def place_slots(name, last_of_chunk, integer, row_out):
            copies((lastd.bitcast(I32) if integer else lastd, last_of_chunk))

            def last_windows(v, ln):
                ln(v.tensor_copy(lastw, lastd.bitcast(I32) if integer else lastd))
                ln(v.tensor_scalar(lastw, lastw, -float(P // 2), 1.0 / P, ALU.add, ALU.mult))
                ln(v.tensor_scalar(lastw, lastw, ROUND, ROUND, ALU.add, ALU.subtract))
                v.tensor_tensor(lastw, lastw, ciota[:, :], ALU.add)
            vector_block(last_windows)
            with nc.Block() as block:
                @block.tensor
                def _(pe):
                    for k in range(2):
                        nc.tensor.matmul(ps[0:SG, k, 0:C // 2], ones[0:1, 0:SG], lastw[:, k * (C // 2):(k + 1) * (C // 2)],
                                         start=True, stop=True)

            def slots(v, ln):
                for g in range(8):
                    c = U[g % 3][:, 0:C]
                    ln(v.tensor_scalar(c.rearrange("p (k n) -> p k n", k=2), ps[0:SG, 0:2, 0:C // 2],
                                       slot_t[:, g:g + 1], None, ALU.is_lt))
                    ln(v.tensor_reduce(slot_c[:, g:g + 1], c, AX, ALU.add))
                ln(v.tensor_scalar(slot_c[:, :], slot_c[:, :], float(C - 1), None, ALU.min))
                ln(v.tensor_copy(slot_ci[:, :], slot_c[:, :]))
                ln(v.tensor_tensor(slot_w[:, :], slot_t[:, :], slot_c[:, :], ALU.subtract))
                ln(v.tensor_scalar(slot_wi[:, :], slot_w[:, :], float(NW - 1), None, ALU.min))
                v.tensor_scalar(slot_w[:, :], slot_w[:, :], float(P), None, ALU.mult)
            vector_block(slots)
            win_tab = dram(f"{name}_windows", [T], I32)
            copies((win_tab.rearrange("(g p) -> p g", p=SG), slot_wi[:, :]))
            copies((row_out[:, :], win_tab.unsqueeze(0)))

        def slot_rows(name, jobs):
            rows_in = sem(f"{name}_gathered")
            with nc.Block() as block:
                @block.gpsimd
                def _(pool):
                    k = 0
                    for o, t in jobs:
                        for g in range(8):
                            nc.gpsimd.indirect_dma_start(o[:, g, :], None, t,
                                                         bass.IndirectOffsetOnAxis(ap=slot_ci[:, g:g + 1], axis=0)
                                                         ).then_inc(rows_in, 16)
                            k += 16
                    pool.wait_ge(rows_in, k)

        def onto_partitions(jobs):
            for i in range(0, len(jobs), 4):
                part = jobs[i:i + 4]
                with nc.Block() as block:
                    @block.tensor
                    def _(pe):
                        for a, (s, d) in enumerate(part):
                            for g in range(8):
                                nc.tensor.transpose(ps[0:P, 2 * a + g // 4, (g % 4) * SG:(g % 4 + 1) * SG],
                                                    s[:, g, :], ident[0:SG, 0:SG])
                with nc.Block() as block:
                    @block.vector
                    def _(dve):
                        for a, (s, d) in enumerate(part):
                            nc.vector.tensor_copy(d.rearrange("p (k n) -> p k n", k=2),
                                                  ps[0:P, 2 * a:2 * a + 2, 0:4 * SG])

        def g3(ap):
            return ap.rearrange("p (g e) -> p g e", e=P)

        place_slots("into", edge_tab[1].rearrange("(c e) -> c e", e=P)[:, P - 1:P].rearrange("c e -> e c"), True, win_row)
        raw = acc[0:SG, 0:5 * 1000].rearrange("p (a n) -> p a n", a=5)
        S, Dst, Ty, Dabs, inwin, base_s, key_s = [acc[0:SG, 5000 + k * 1000:6000 + k * 1000] for k in range(7)]
        slot_rows("into", [(g3(raw[:, a, :] if a > 2 else raw[:, a, :].bitcast(I32)), t.rearrange("(c e) -> c e", e=P))
                           for a, t in enumerate(edge_tab)])

        def edges1(v, ln):
            ln(v.tensor_copy(S, raw[:, 0, :].bitcast(I32)))
            ln(v.tensor_copy(Dabs, raw[:, 1, :].bitcast(I32)))
            ln(v.tensor_copy(Ty, raw[:, 2, :].bitcast(I32)))
            ln(v.tensor_tensor(g3(Dst), g3(Dabs), bf(slot_w[:, :], P), ALU.subtract))
            ln(v.tensor_scalar(inwin, Dst, 0.0, None, ALU.is_ge))
            ln(v.scalar_tensor_tensor(inwin, Dst, float(P - 1), inwin, ALU.is_le, ALU.mult))
            ln(v.scalar_tensor_tensor(Ty, S, float(NT), Ty, ALU.mult, ALU.add))
            ln(v.tensor_scalar(key_s, S, -float(P // 2), 1.0 / P, ALU.add, ALU.mult))
            ln(v.tensor_scalar(key_s, key_s, ROUND, ROUND, ALU.add, ALU.subtract))
            ln(v.scalar_tensor_tensor(key_s, key_s, -float(NW), inwin, ALU.add, ALU.mult))
            ln(v.tensor_scalar(key_s, key_s, float(NW), None, ALU.add))
            ln(v.tensor_scalar(U[0], raw[:, 4, :], dcol[:, 0:1], dcol[:, 1:2], ALU.mult, ALU.add))
            v.scalar_tensor_tensor(U[1], U[0], -1.0, U[0], ALU.mult, ALU.max)
        vector_block(edges1)
        with nc.Block() as block:
            @block.scalar
            def _(act):
                link(act, nc.scalar.activation(U[1], U[1], ACT.Exp, scale=-1.0), act_ch)
                nc.scalar.activation(U[2], U[1], ACT.Ln, bias=1.0)

        def edges2(v, ln):
            ln(v.tensor_tensor(inwin, S, Dabs, ALU.not_equal))
            ln(v.scalar_tensor_tensor(U[2], U[0], 0.0, U[2], ALU.max, ALU.add))
            ln(v.tensor_tensor(base_s, U[2], raw[:, 3, :], ALU.mult))
            v.tensor_tensor(base_s, base_s, inwin, ALU.mult)
        vector_block(edges2)
        rec3 = REC[:, 0:T * 3].rearrange("p (c f) -> p c f", f=3)
        onto_partitions([(g3(Dst), dloc[:, :]), (g3(Ty), typed_idx[:, 0:T]), (g3(key_s), key),
                         (g3(S), rec3[:, :, 0]), (g3(Dabs), rec3[:, :, 1]), (g3(base_s), rec3[:, :, 2])])

        counts = dram("counts", [NW, P, N])
        NB = (NW + 3) // 4
        src_cols = arena[0:P, 10700:10700 + C + 2]
        dst_cols = arena[0:P, 11502:11502 + C + 2]
        iota_src = arena[0:P, 6000:7564].bitcast(I16)
        hot_src = [arena[0:P, 7564 + k * 1564:9128 + k * 1564].bitcast(BF16) for k in range(2)]
        small16 = arena[0:P, 12304:12304 + 4 * 64]
        hot_dst = [small16[:, k * 64:(k + 1) * 64].bitcast(BF16) for k in range(2)]
        iota_dst = small16[:, 128:192].bitcast(I16)
        zeros = arena[0:P, 12560:12560 + 250].bitcast(BF16)
        finished = acc[:, 0:N]
        ranges = acc[0:1, 12700:12700 + 3 * NW].bitcast(I32)
        CH2 = C // 8
        lists2 = acc[0:CH2, 0:2000].rearrange("p (a g e) -> p a g e", a=2, e=P)
        floats2 = acc[0:CH2, 2000:4000].rearrange("p (a g e) -> p a g e", a=2, e=P)
        ends = acc[0:1, 4000:4000 + 2 * C].rearrange("p (a c) -> p a c", a=2)
        endw = acc[0:1, 6000:6000 + 2 * C].rearrange("p (a c) -> p a c", a=2)
        below = acc[0:NW, 8000:8000 + 2 * C].rearrange("p (a c) -> p a c", a=2)
        span = acc[0:NW, 9800:9808]
        span_i = acc[0:NW, 9820:9823].bitcast(I32)
        chunk_dst = edge_tab[1].rearrange("(c e) -> c e", e=P)
        copies(*[(lists2[:, a].bitcast(I32), edge_tab[a].rearrange("(g p e) -> p g e", p=CH2, e=P)) for a in range(2)],
               (ends[:, 0, :].bitcast(I32), chunk_dst[:, P - 1:P].rearrange("c e -> e c")),
               (ends[:, 1, :].bitcast(I32), chunk_dst[:, 0:1].rearrange("c e -> e c")))

        def chunk_ends(v, ln):
            v.tensor_copy(floats2, lists2.bitcast(I32))
            ln(v.tensor_copy(endw, ends.bitcast(I32)))
            ln(v.tensor_scalar(endw, endw, -float(P // 2), 1.0 / P, ALU.add, ALU.mult))
            v.tensor_scalar(endw, endw, ROUND, ROUND, ALU.add, ALU.subtract)
        vector_block(chunk_ends)
        with nc.Block() as block:
            @block.tensor
            def _(pe):
                for a in range(2):
                    for g in range(8):
                        nc.tensor.transpose(ps[0:P, 2 * a + g // 4, (g % 4) * CH2:(g % 4 + 1) * CH2],
                                            floats2[:, a, g, :], ident[0:CH2, 0:CH2])
                    for k in range(2):
                        nc.tensor.matmul(ps[0:NW, 4 + 2 * a + k, 0:C // 2], ones[0:1, 0:NW],
                                         endw[:, a, k * (C // 2):(k + 1) * (C // 2)], start=True, stop=True)

            @block.gpsimd
            def _(pool):
                nc.gpsimd.iota(iota_src, [[1, N + 3]], base=0, channel_multiplier=0)

        def spans(v, ln):
            halves = lambda t: t.rearrange("p (k n) -> p k n", k=2)
            for a, t in enumerate((src_cols, dst_cols)):
                v.tensor_copy(halves(t[:, 0:C]), ps[0:P, 2 * a:2 * a + 2, 0:4 * CH2])
                v.memset(t[:, C:C + 2], -1.0)
            v.tensor_scalar(halves(below[:, 0, :]), ps[0:NW, 4:6, 0:C // 2], slot_t[0:NW, 0:1], None, ALU.is_lt)
            ln(v.tensor_scalar(halves(below[:, 1, :]), ps[0:NW, 6:8, 0:C // 2], slot_t[0:NW, 0:1], None, ALU.is_le))
            ln(v.tensor_reduce(span[:, 0:2], below, AX, ALU.add))
            ln(v.tensor_tensor(span[:, 2:3], span[:, 1:2], span[:, 0:1], ALU.subtract))
            ln(v.tensor_scalar(span[:, 2:3], span[:, 2:3], 1.0, None, ALU.max))
            ln(v.tensor_scalar(span[:, 0:1], span[:, 0:1], float(C - 1), None, ALU.min))
            ln(v.tensor_scalar(span[:, 2:3], span[:, 2:3], 0.5, 0.25, ALU.mult, ALU.add))
            v.tensor_scalar(span[:, 2:3], span[:, 2:3], ROUND, ROUND, ALU.add, ALU.subtract)
        vector_block(spans)
        with nc.Block() as block:
            @block.tensor
            def _(pe):
                nc.tensor.matmul(ps[0:NW, 0, 0:1], before[0:NW, 0:NW], span[:, 2:3], start=True, stop=True)

        def steps_of(v, ln):
            ln(v.tensor_copy(span[:, 3:4], ps[0:NW, 0, 0:1]))
            v.tensor_tensor(span[:, 4:5], span[:, 3:4], span[:, 2:3], ALU.add)
            ln(v.scalar_tensor_tensor(span[:, 5:6], span[:, 3:4], 2.0, span[:, 0:1], ALU.mult, ALU.subtract))
            v.tensor_copy(span_i, span[:, 3:6])
        vector_block(steps_of)
        range_tab = dram("ranges", [3, NW], I32)
        copies((range_tab.rearrange("k w -> w k"), span_i))
        copies((ranges, range_tab.rearrange("k w -> (k w)").unsqueeze(0)))

        def counting():
            hot, hot_free, done, by_act, by_dve, stored, moved_on = [sem(f"count_{n}") for n in
                ("onehots", "onehots_free", "window_summed", "banks_of_act", "banks_of_dve", "stored", "next_window")]
            NA = 4

            def bounds(eng, w, which):
                return [eng.value_load(ranges[0:1, ds(w + k * NW, 1)], min_val=lo, max_val=hi)
                        for k, lo, hi in which]
            first, end, less = (0, 0, 440), (1, 1, 440), (2, 0, 880)

            def vector(dve):
                v = nc.vector
                v.memset(hot_src[0], 0.0).then_inc(hot_free, 2)
                v.memset(slotv[:, 0, 0:1], 0.0).then_inc(by_act, NA)
                v.memset(slotv[:, 1, 0:1], 0.0).then_inc(by_dve, NB - NA)
                v.memset(zeros, 0.0).then_inc(stored, 16)
                v.tensor_copy(iota_dst[:, 0:P], iota_src[:, 0:P]).then_inc(moved_on, 1)
                dve.wait_ge(moved_on, 1)
                with dve.Fori(0, NW) as w:
                    i0, i1, off = bounds(dve, w, (first, end, less))
                    with dve.Fori(i0, i1) as i:
                        for k in range(2):
                            c = nc.s_assert_within(dve.snap(i * 2 + k - off), min_val=0, max_val=C + 1,
                                                   skip_runtime_bounds_check_because="ranges of chunks")
                            dve.wait_ge(hot_free, i * 2 + k + 1)
                            v.tensor_scalar(hot_src[k][:, 0:N + 3], iota_src[:, 0:N + 3], src_cols[:, ds(c, 1)], None,
                                            ALU.is_equal)
                            v.tensor_scalar(hot_dst[k][:, 0:P], iota_dst[:, 0:P], dst_cols[:, ds(c, 1)], None,
                                            ALU.is_equal).then_inc(hot, 1)
                    v.tensor_scalar(iota_dst[:, 0:P], iota_dst[:, 0:P], float(P), None, ALU.add).then_inc(moved_on, 1)
                    dve.wait_ge(moved_on, w + 2)
                    dve.wait_ge(done, w + 1)
                    dve.wait_ge(stored, w * 16 + 16)
                    for j in range(NA, NB):
                        n = min(4, NW - 4 * j) * P
                        v.tensor_copy(finished[:, j * 4 * P:j * 4 * P + n], ps[0:P, j, 0:n]).then_inc(by_dve, 1)

            def tensor(pe):
                pe.wait_ge(stored, 16)
                with pe.Fori(0, NW) as w:
                    i0, i1 = bounds(pe, w, (first, end))
                    for j in range(NB):
                        n = min(4, NW - 4 * j) * P
                        if j < NA:
                            pe.wait_ge(by_act, w * NA + j + 1)
                        else:
                            pe.wait_ge(by_dve, w * (NB - NA) + j - NA + 1)
                        nc.tensor.matmul(ps[:, j, 0:n], zeros[:, 0:128], zeros[:, 0:n], start=True, stop=False,
                                         skip_group_check=True)
                    with pe.Fori(i0, i1) as i:
                        for k in range(2):
                            pe.wait_ge(hot, i * 2 + k + 1)
                            for b in range(NW):
                                last = nc.tensor.matmul(ps[:, b // 4, (b % 4) * P:(b % 4 + 1) * P],
                                                        hot_src[k][:, b * P:b * P + 128], hot_dst[k][:, 0:P],
                                                        start=False, stop=False, skip_group_check=True)
                            last.then_inc(hot_free, 1)
                    for j in range(NB):
                        last = nc.tensor.matmul(ps[:, j, 0:64], zeros[:, 0:128], zeros[:, 0:64], start=False, stop=True,
                                                skip_group_check=True)
                    last.then_inc(done, 1)

            def scalar(act):
                with act.Fori(0, NW) as w:
                    act.wait_ge(done, w + 1)
                    act.wait_ge(stored, w * 16 + 16)
                    for j in range(NA):
                        nc.scalar.activation(finished[:, j * 4 * P:(j + 1) * 4 * P], ps[0:P, j, 0:4 * P],
                                             ACT.Copy).then_inc(by_act, 1)

            def sync(sp):
                with sp.Fori(0, NW) as w:
                    sp.wait_ge(by_act, w * NA + 2 * NA)
                    sp.wait_ge(by_dve, w * (NB - NA) + 2 * (NB - NA))
                    sp.dma_start(counts[ds(w, 1)].rearrange("w p n -> p (w n)"), finished).then_inc(stored, 16)
                sp.wait_ge(stored, 16 * (NW + 1))
            return dict(vector=vector, tensor=tensor, scalar=scalar, sync=sync)

        cos_tab = dram("by_source", [T * P, 3])
        bucket("by_source", T, NW + 1, REC, 3, cos_tab, None, beside=counting())
        cos_rows = cos_tab.rearrange("(c e) f -> c (e f)", e=P)
        place_slots("out_of", cos_rows[0:C, 3 * (P - 1):3 * (P - 1) + 1].rearrange("c e -> e c"), False, cos_win_row)
        raw3 = acc[0:SG, 0:3000].rearrange("p (g m) -> p g m", g=8)
        raw3v = raw3.rearrange("p g (e f) -> p g e f", f=3)
        slot_rows("out_of", [(raw3, cos_rows)])
        Sl, In, Ba, De = [g3(acc[0:SG, 5000 + k * 1000:6000 + k * 1000]) for k in range(4)]

        def edges3(v, ln):
            ln(v.tensor_tensor(Sl, raw3v[:, :, :, 0], bf(slot_w[:, :], P), ALU.subtract))
            ln(v.tensor_copy(De, raw3v[:, :, :, 1]))
            v.tensor_copy(Ba, raw3v[:, :, :, 2])
        vector_block(edges3)
        onto_partitions([(Sl, sloc[:, :]), (De, cos_idx[:, 0:T]), (Ba, base_w[:, :])])

        def pad(v, ln):
            v.memset(typed_idx[:, T:T + G], 0)
            v.memset(cos_idx[:, T:T + G], 0)
        vector_block(pad)

        def windows(g, row_of=win_row):
            return nc.values_load_multi_w_load_instructions(
                row_of[0:1, ds(g * G, G)], engines=(mybir.EngineType.DVE,), min_val=0, max_val=NW - 1,
                skip_runtime_bounds_check_because="bounded where the slots are laid out")[1]

        def to_rows(v, out_ap, col, g, width=P):
            return v.tensor_tensor(out_ap, iota_row[:, 0:width].unsqueeze(1).to_broadcast([P, G, width]),
                                   bf(col[:, ds(g * G, G)], width), ALU.is_equal)

        def gather_engine(name, pool, table, idx, width, arrived, used):
            listed = sem(f"{name}_indices")

            nc.gpsimd.tensor_copy(group_idx[:, 0, :], idx[:, 0:G]).then_inc(listed, 1)

            def step(g, k):
                pool.wait_ge(listed, g + 1)
                if after(g, 3):
                    pool.wait_ge(used, g - 2)
                nc.gpsimd.tensor_copy(group_idx[:, (k + 1) % 4, :], idx[:, ds((g + 1) * G, G)]).then_inc(listed, 1)
                for j in range(G):
                    nc.gpsimd.indirect_dma_start(gath[:, k, :, :].rearrange("p j f -> p (j f)")[:, j * width:(j + 1) * width],
                                                 None, table,
                                                 bass.IndirectOffsetOnAxis(ap=group_idx[:, k, j:j + 1], axis=0)
                                                 ).then_inc(arrived[k], 16)
            run(pool, step, 0)

        def sum_pass(name, table, idx):
            arrived = [sem(f"{name}_rows{k}") for k in range(4)]
            hot = sem(f"{name}_onehot")
            summed = sem(f"{name}_slot_sums")
            added = sem(f"{name}_added")
            vector_block(lambda v, ln: v.memset(acc[:, 0:NW * D], 0.0))
            with nc.Block() as block:
                @block.gpsimd
                def _(pool):
                    gather_engine(name, pool, table, idx, D, arrived, summed)

                @block.tensor
                def _(pe):
                    def step(g, k):
                        pe.wait_ge(hot, g + 1)
                        pe.wait_ge(arrived[k], full(g, k))
                        if after(g, 2):
                            pe.wait_ge(added, (g - 1) * G)
                        for j in range(G):
                            last = nc.tensor.matmul(ps[0:P, k % 2, j * D:(j + 1) * D], onehot[:, k, j, :],
                                                    rows_of(k, D)[:, j, :], start=True, stop=True)
                        last.then_inc(summed, 1)
                    run(pe, step, 0)

                @block.vector
                def _(dve):
                    def step(g, k):
                        if not isinstance(g, int) or g < NG:
                            if after(g, 4):
                                dve.wait_ge(summed, g - 3)
                            to_rows(nc.vector, onehot[:, k, :, :], dloc, g).then_inc(hot, 1)
                        if after(g, 1):
                            w = windows(g - 1)
                            dve.wait_ge(summed, g)
                            for j in range(G):
                                if after(g, 2) or j:
                                    dve.wait_ge(added, (g - 1) * G + j)
                                a = acc[:, ds(w[j] * D, D)]
                                nc.vector.tensor_tensor(a, a, ps[0:P, (k + 1) % 2, j * D:(j + 1) * D], ALU.add
                                                        ).then_inc(added, 1)
                    run(dve, step, 1)

        GW = NW // WG

        def load_pieces(sp, g, nw, arrived, ready_to_load):
            for q in range(PT):
                ready_to_load(q)
                sp.dma_start(pieces[q][:, 0:nw, :, :].rearrange("p w b d -> p w (b d)"),
                             counts[ds(g * WG, nw), :, q * PT * P:(q + 1) * PT * P].rearrange("w p m -> p w m")
                             ).then_inc(arrived[q], 16)

        def group_pairs(eng, step, peel=0):
            for g in range(2 * peel):
                step(g, g % 2, WG)
            with eng.Fori(peel, GW // 2) as i:
                for k in range(2):
                    step(i * 2 + k, k, WG)
            step(GW, GW % 2, NW - GW * WG)

        def mean_pass(name, rows, sums):
            F1 = D + 1
            arrived = [sem(f"{name}_piece{q}") for q in range(PT)]
            summed, banks = sem(f"{name}_piece_summed"), sem(f"{name}_banks_free")
            with nc.Block() as block:
                @block.sync
                def _(sp):
                    def step(g, k, nw):
                        def wait(q):
                            if after(g, 1):
                                sp.wait_ge(summed, g * PT - PT + q + 1)
                        load_pieces(sp, g, nw, arrived, wait)
                    group_pairs(sp, step, peel=1)

                @block.tensor
                def _(pe):
                    def step(g, k, nw):
                        pe.wait_ge(banks, g + 1)
                        for b in range(NW):
                            if b % PT == 0:
                                pe.wait_ge(arrived[b // PT], g * 16 + 16)
                            for w in range(nw):
                                last = nc.tensor.matmul(ps[0:P, k, w * F1:(w + 1) * F1], pieces[b // PT][:, w, b % PT, :],
                                                        rows[:, b, :], start=(b == 0 and w == 0),
                                                        stop=(b == NW - 1 and w == nw - 1), skip_group_check=True)
                            if b % PT == PT - 1:
                                last.then_inc(summed, 1)
                    group_pairs(pe, step)

                @block.vector
                def _(dve):
                    nc.vector.memset(slotv[:, 0, 0:1], 0.0).then_inc(banks, 2)

                    def step(g, k, nw):
                        dve.wait_ge(summed, g * PT + PT)
                        nc.vector.tensor_copy(sums[:, ds(g * WG, nw), :], ps[0:P, k, 0:nw * F1].rearrange(
                            "p (w f) -> p w f", f=F1)).then_inc(banks, 1)
                    group_pairs(dve, step)

        def attention_pass(name, rows, F, H, q_src, r_tab):
            F1 = F + 1
            S = NW * H
            R = 4 if H == 4 else 5
            arrived = [sem(f"{name}_piece{q}") for q in range(PT)]
            r_in = [sem(f"{name}_r{k}") for k in range(2)]
            excess, weights, summed, banks = [sem(f"{name}_{n}") for n in
                ("excess", "weights", "step_summed", "banks_free")]
            r_rows = [hflat[:, k * 1500:k * 1500 + WG * H * P].rearrange("p (w h d) -> p w h d", h=H, d=P) for k in range(2)]
            over = [tmp[0:P, k * WG * P:(k + 1) * WG * P] for k in range(R)]
            wt_at = tmp[0:P, 1500:3000] if H == 4 else arena[0:P, 6000:6000 + R * WG * P]
            wt = [wt_at[:, k * WG * P:(k + 1) * WG * P] for k in range(R)]
            with nc.Block() as block:
                @block.sync
                def _(sp):
                    def step(g, k, nw):
                        if after(g, 2):
                            sp.wait_ge(excess, g * S - S)
                        sp.dma_start(r_rows[k][:, 0:nw, :, :].rearrange("p w h d -> p (w h d)"),
                                     r_tab[ds(g * (WG * H * P), nw * H * P)].unsqueeze(0).to_broadcast([P, nw * H * P])
                                     ).then_inc(r_in[k], 16)

                        def wait(q):
                            if after(g, 1):
                                sp.wait_ge(weights, g * S - S + (q + 1) * PT * H + R)
                        load_pieces(sp, g, nw, arrived, wait)
                    group_pairs(sp, step, peel=1)

                @block.scalar
                def _(act):
                    def step(g, k, nw):
                        half = g // 2 if isinstance(g, int) else None
                        if half is None:
                            act.wait_ge(r_in[k], (g - k) * 8 + 16)
                        else:
                            act.wait_ge(r_in[k], half * 16 + 16)
                        for b in range(NW):
                            for a in range(H):
                                n = b * H + a
                                act.wait_ge(weights, g * S + n + 1)
                                nc.scalar.activation(over[n % R][:, 0:nw * P].rearrange("p (w d) -> p w d", d=P),
                                                     r_rows[k][:, 0:nw, a, :], ACT.Relu, scale=q_src[:, b, a:a + 1],
                                                     bias=minus_one[:, 0:1]).then_inc(excess, 1)
                    group_pairs(act, step)

                @block.tensor
                def _(pe):
                    def step(g, k, nw):
                        for b in range(NW):
                            for a in range(H):
                                n = b * H + a
                                if b == 0:
                                    pe.wait_ge(banks, g * H + a + 1)
                                pe.wait_ge(weights, g * S + n + 1 + R)
                                for w in range(nw):
                                    last = nc.tensor.matmul(ps[0:P, 4 * k + a, w * F1:(w + 1) * F1],
                                                            wt[n % R][:, w * P:(w + 1) * P], rows[:, b, a, :],
                                                            start=(b == 0 and w == 0),
                                                            stop=(b == NW - 1 and w == nw - 1), skip_group_check=True)
                                last.then_inc(summed, 1)
                    group_pairs(pe, step)

                @block.vector
                def _(dve):
                    v = nc.vector
                    v.memset(slotv[:, 0, 0:1], 0.0).then_inc(weights, R)
                    v.memset(slotv[:, 1, 0:1], 0.0).then_inc(summed, R)
                    v.memset(slotv[:, 2, 0:1], 0.0).then_inc(banks, 2 * H)

                    def read_banks(g, k, nw):
                        a_g = acc[:, ds(g * (WG * H * F1), nw * H * F1)].rearrange("p (w m) -> p w m", w=nw)
                        for a in range(H):
                            dve.wait_ge(summed, g * S + (NW - 1) * H + a + 1 + R)
                            o = a_g[:, :, a * F1:(a + 1) * F1]
                            v.tensor_tensor(o, o, ps[0:P, 4 * k + a, 0:nw * F1].rearrange("p (w f) -> p w f", f=F1),
                                            ALU.add).then_inc(banks, 1)

                    def step(g, k, nw):
                        for b in range(NW):
                            for a in range(H):
                                n = b * H + a
                                if n == 2 * R and k == 1:
                                    read_banks(g - 1, 0, WG)
                                if b % PT == 0 and a == 0:
                                    dve.wait_ge(arrived[b // PT], g * 16 + 16)
                                dve.wait_ge(excess, g * S + n + 1)
                                dve.wait_ge(summed, g * S + n + 1)
                                v.scalar_tensor_tensor(wt[n % R][:, 0:nw * P].rearrange("p (w d) -> p w d", d=P),
                                                       over[n % R][:, 0:nw * P].rearrange("p (w d) -> p w d", d=P), 1.0,
                                                       pieces[b // PT][:, 0:nw, b % PT, :], ALU.add, ALU.mult
                                                       ).then_inc(weights, 1)
                        if k == 1 or nw < WG:
                            read_banks(g, k, nw)
                    group_pairs(dve, step)

        def gat(name, X, F, H, CH, W, a_s, a_d, bias, out_ap):
            F1 = F + 1
            MW = H * F1
            HC = H * CH
            t1, t2 = tmp[0:F, 0:HC], tmp[0:F, 512:512 + HC]
            copies((wts[0:F, 0:HC], W), (t1, row(a_s.rearrange("h c -> (h c)"), F)),
                   (t2, row(a_d.rearrange("h c -> (h c)"), F)), (vecs[:, 0:CH], row(bias)))

            def att(v, ln):
                for k, t in enumerate((t1, t2)):
                    ln(v.tensor_tensor(t, t, wts[0:F, 0:HC], ALU.mult))
                    ln(v.tensor_reduce(watt[0:F, k * H:(k + 1) * H], t.rearrange("p (h c) -> p h c", c=CH), AX, ALU.add))
            vector_block(att)
            node_transpose([(lambda w: X[:, w, :], F, xT)])
            node_matmul([(window_of(xT, F), watt[0:F, 0:2 * H])], 2 * H,
                        lambda v, w, n: nc.vector.tensor_copy(alpha[:, w:w + n, 0:2 * H], v))
            vector_block(lambda v, ln: v.tensor_reduce(slotv[:, 15, 0:H], alpha[:, :, 0:H].rearrange("p w h -> p h w"),
                                                       AX, ALU.max))
            with nc.Block() as block:
                @block.gpsimd
                def _(pool):
                    nc.gpsimd.partition_all_reduce(alpha_max[:, 0:H], slotv[:, 15, 0:H], P, RMAX)
            u, q, r, own = [tmp[0:P, k * 100:k * 100 + NW * H].rearrange("p (w h) -> p w h", h=H) for k in range(4)]
            q_keep = slotv.rearrange("p a b -> p (a b)")[:, 100:100 + NW * H].rearrange("p (w h) -> p w h", h=H)
            peak = bw(alpha_max[:, 0:H])

            def terms(v, ln):
                v.tensor_tensor(u, alpha[:, :, 0:H], peak, ALU.subtract)
                ln(v.tensor_tensor(r, alpha[:, :, H:2 * H], peak, ALU.add))
                v.tensor_scalar(r, r, 1.0 - SLOPE, 80.0, ALU.mult, ALU.min)
            vector_block(terms)
            with nc.Block() as block:
                @block.scalar
                def _(act):
                    nc.scalar.activation(q_keep, u, ACT.Exp, scale=1.0 - SLOPE)
                    nc.scalar.activation(q, u, ACT.Exp, scale=SLOPE)
                    nc.scalar.activation(own, r, ACT.Exp)
            u, r, own = q, own, u
            rows = arena[0:P, 0:NW * MW].rearrange("p (w h f) -> p w h f", h=H, f=F1)
            accv = acc[:, 0:NW * MW].rearrange("p (w h f) -> p w h f", h=H, f=F1)
            r_turned = tmp[0:NW * H, 500:500 + P]
            with nc.Block() as block:
                @block.tensor
                def _(pe):
                    nc.tensor.transpose(ps[0:NW * H, 0, 0:P], r.rearrange("p w h -> p (w h)"), ident[0:P, 0:P])

            def seed(v, ln):
                v.tensor_copy(r_turned, ps[0:NW * H, 0, 0:P])
                ln(v.tensor_tensor(own, q_keep, r, ALU.mult))
                v.tensor_scalar(own, own, 1.0, None, ALU.max)
                for a in range(H):
                    v.tensor_tensor(rows[:, :, a, 0:F], X, bf(u[:, :, a], F), ALU.mult)
                ln(v.tensor_copy(rows[:, :, :, F], u))
                for a in range(H):
                    v.tensor_tensor(accv[:, :, a, :], rows[:, :, a, :], bf(own[:, :, a], F1), ALU.mult)
            vector_block(seed)
            r_tab = dram(f"{name}_r", [NW * H * P])
            copies((r_tab.rearrange("(k p) -> k p", p=P), r_turned))
            attention_pass(name, rows, F, H, q_keep, r_tab)

            def divide(v, ln):
                den = tmp[0:P, 0:NW * H].rearrange("p (w h) -> p w h", h=H)
                ln(v.reciprocal(den, accv[:, :, :, F]))
                for a in range(H):
                    c = accv[:, :, a, 0:F]
                    v.tensor_tensor(c, c, bf(den[:, :, a], F), ALU.mult)
            vector_block(divide)
            node_transpose([(lambda w, a=a: accv[:, w, a, 0:F], F, tT[a]) for a in range(H)])
            node_matmul([(window_of(tT[a], F), wts[0:F, a * CH:(a + 1) * CH]) for a in range(H)], CH,
                        lambda v, w, n: nc.vector.scalar_tensor_tensor(
                            out_ap[:, w:w + n, :], v, 1.0 / H,
                            vecs[:, 0:CH].unsqueeze(1).to_broadcast([P, n, CH]), ALU.mult, ALU.add))

        def norm_elu(gamma, beta):
            hsq = tmp[0:P, :].rearrange("p (w f) -> p w f", f=128)
            copies((vecs[:, 0:128], row(gamma)), (vecs[:, 128:256], row(beta)))
            column_sums(lambda w: h[:, w, :], stat[:, 0, :])

            def centre(v, ln):
                ln(v.tensor_scalar(stat[:, 0, :], stat[:, 0, :], 1.0 / N, None, ALU.mult))
                ln(v.tensor_tensor(h[:, :, :], h[:, :, :], bw(stat[:, 0, :]), ALU.subtract))
                v.tensor_tensor(hsq, h[:, :, :], h[:, :, :], ALU.mult)
            vector_block(centre)
            column_sums(lambda w: hsq[:, w, :], stat[:, 1, :])
            vector_block(lambda v, ln: v.tensor_scalar(stat[:, 1, :], stat[:, 1, :], 1.0 / N, BN_EPS, ALU.mult, ALU.add))
            scalar_fn(stat[:, 2, :], stat[:, 1, :], ACT.Sqrt)

            def scale(v, ln):
                ln(v.reciprocal(stat[:, 3, :], stat[:, 2, :]))
                ln(v.tensor_tensor(stat[:, 3, :], stat[:, 3, :], vecs[:, 0:128], ALU.mult))
                ln(v.tensor_tensor(h[:, :, :], h[:, :, :], bw(stat[:, 3, :]), ALU.mult))
                ln(v.tensor_tensor(h[:, :, :], h[:, :, :], bw(vecs[:, 128:256]), ALU.add))
                v.tensor_scalar(hsq, h[:, :, :], 0.0, None, ALU.min)
            vector_block(scale)
            scalar_fn(hsq, hsq, ACT.Exp)

            def elu(v, ln):
                ln(v.tensor_scalar(hsq, hsq, -1.0, None, ALU.add))
                v.scalar_tensor_tensor(h[:, :, :], h[:, :, :], 0.0, hsq, ALU.max, ALU.add)
            vector_block(elu)

        h64 = h[:, :, 0:D]

        gat("gat1", x[:, :, :], D, 4, 128, W1, as1, ad1, b1, h[:, :, :])
        norm_elu(g1, be1)
        gat("gat2", h[:, :, :], 128, 4, 128, W2, as2, ad2, b2, h[:, :, :])
        norm_elu(g2, be2)
        gat("gat3", h[:, :, :], 128, 1, D, W3, as3, ad3, b3, h64)
        vector_block(lambda v, ln: v.tensor_tensor(x[:, :, :], x[:, :, :], h64, ALU.add))
        layernorm(x[:, :, :])

        cur = h[:, :, D:2 * D]
        vector_block(lambda v, ln: v.tensor_copy(cur[:, :, :], x[:, :, :]))
        accD = acc[:, 0:NW * D].rearrange("p (w f) -> p w f", f=D)
        cur1 = arena[0:P, 6 * 1000:6 * 1000 + NW * (D + 1)].rearrange("p (w f) -> p w f", f=D + 1)
        sums = acc[:, 0:NW * (D + 1)].rearrange("p (w f) -> p w f", f=D + 1)
        accN = acc[:, 2000:2000 + NW * D].rearrange("p (w f) -> p w f", f=D)
        vector_block(lambda v, ln: v.memset(cur1[:, :, D:D + 1], 1.0))
        for l in range(3):
            vector_block(lambda v, ln: v.tensor_copy(cur1[:, :, 0:D], cur))
            copies((wts[0:D, 0:D], W_self[l]), (wts[0:D, D:2 * D], W_neigh[l]), (vecs[:, 0:D], row(b_sage[l])))
            mean_pass(f"sage{l}", cur1, sums)

            def mean(v, ln):
                if l == 0:
                    ln(v.tensor_scalar(inv_deg[:, :], sums[:, :, D], 1.0, None, ALU.max))
                    ln(v.reciprocal(inv_deg[:, :], inv_deg[:, :]))
                v.tensor_tensor(accN, sums[:, :, 0:D], bf(inv_deg[:, :], D), ALU.mult)
            vector_block(mean)
            node_transpose([(lambda w: cur[:, w, :], D, tT[0]), (lambda w: accN[:, w, :], D, tT[1])])
            node_matmul([(window_of(tT[0], D), wts[0:D, 0:D]), (window_of(tT[1], D), wts[0:D, D:2 * D])], D,
                        lambda v, w, n: nc.vector.tensor_tensor(
                            cur[:, w:w + n, :], v, vecs[:, 0:D].unsqueeze(1).to_broadcast([P, n, D]), ALU.add))
            if l < 2:
                vector_block(lambda v, ln: v.tensor_scalar(cur[:, :, :], cur[:, :, :], 0.0, None, ALU.max))
        vector_block(lambda v, ln: v.tensor_tensor(x[:, :, :], x[:, :, :], cur[:, :, :], ALU.add))
        layernorm(x[:, :, :])

        typed = dram("typed_table", [N * NT, D])
        emn = tmp[:, 0:4 * D].rearrange("p (k h) -> p k h", h=D)
        ihn = tmp[0:96, 256:256 + 2 * D].rearrange("p (k h) -> p k h", h=D)
        hhn = tmp[0:96, 384:384 + 2 * D].rearrange("p (k h) -> p k h", h=D)
        emT = wts[0:D, 0:NT * D]
        gateT = tmp[0:D, 1024:1024 + 6 * D].rearrange("p (k g) -> p k g", k=2)
        copies((emn, edge_matrix.rearrange("t (m h) -> (t m) h", h=D).rearrange("(k p) h -> p k h", p=128)),
               (ihn, w_ih.rearrange("(k p) h -> p k h", p=96)), (hhn, w_hh.rearrange("(k p) h -> p k h", p=96)),
               (vecs[:, 0:3 * D], row(b_ih)), (vecs[:, 3 * D:6 * D], row(b_hh)))
        with nc.Block() as block:
            @block.tensor
            def _(pe):
                for k in range(4):
                    nc.tensor.transpose(ps[0:D, 0, k * 128:(k + 1) * 128], emn[:, k, :], ident[:, :])
                for k in range(2):
                    nc.tensor.transpose(ps[0:D, 1, k * 96:(k + 1) * 96], ihn[:, k, :], ident[0:96, 0:96])
                    nc.tensor.transpose(ps[0:D, 2, k * 96:(k + 1) * 96], hhn[:, k, :], ident[0:96, 0:96])

        def keep(v, ln):
            v.tensor_copy(emT, ps[0:D, 0, :])
            v.tensor_copy(gateT[:, 0, :], ps[0:D, 1, 0:3 * D])
            v.tensor_copy(gateT[:, 1, :], ps[0:D, 2, 0:3 * D])
        vector_block(keep)
        node_transpose([(lambda w: x[:, w, :], D, tT[0])])
        typed_sb = acc[:, 0:NW * NT * D].rearrange("p (w m) -> p w m", w=NW)
        node_matmul([(window_of(tT[0], D), emT)], NT * D,
                    lambda v, w, n: nc.vector.tensor_copy(typed_sb[:, w:w + n, :], v))
        copies((typed.rearrange("(w p t) f -> p w (t f)", p=P, t=NT), typed_sb))
        sum_pass("ggnn", typed, typed_idx)
        gates = arena[0:P, 2 * N:2 * N + NW * 192].rearrange("p (w g) -> p w g", g=192)
        node_transpose([(lambda w: x[:, w, :], D, tT[0]), (lambda w: accD[:, w, :], D, tT[1])])

        def biases(v, ln):
            v.tensor_tensor(vecs[:, 512:512 + 2 * D], vecs[:, 0:2 * D], vecs[:, 3 * D:5 * D], ALU.add)
            v.tensor_copy(vecs[:, 512 + 2 * D:512 + 3 * D], vecs[:, 2 * D:3 * D])
        vector_block(biases)
        node_matmul([(window_of(tT[1], D), gateT[:, 0, 0:2 * D]), (window_of(tT[0], D), gateT[:, 1, 0:2 * D])], 2 * D,
                    lambda v, w, n: nc.vector.tensor_tensor(
                        gates[:, w:w + n, 0:2 * D], v,
                        vecs[:, 512:512 + 2 * D].unsqueeze(1).to_broadcast([P, n, 2 * D]), ALU.add))
        node_matmul([(window_of(tT[1], D), gateT[:, 0, 2 * D:3 * D])], D,
                    lambda v, w, n: nc.vector.tensor_tensor(
                        gates[:, w:w + n, 2 * D:3 * D], v,
                        vecs[:, 2 * D:3 * D].unsqueeze(1).to_broadcast([P, n, D]), ALU.add))
        node_matmul([(window_of(tT[0], D), gateT[:, 1, 2 * D:3 * D])], D,
                    lambda v, w, n: nc.vector.tensor_tensor(
                        cur[:, w:w + n, :], v,
                        vecs[:, 5 * D:6 * D].unsqueeze(1).to_broadcast([P, n, D]), ALU.add))
        scalar_fn(gates[:, :, 0:2 * D], gates[:, :, 0:2 * D], ACT.Sigmoid)
        r_g, z_g, n_g = (gates[:, :, k * D:(k + 1) * D] for k in range(3))

        def fresh(v, ln):
            ln(v.tensor_tensor(cur[:, :, :], cur[:, :, :], r_g, ALU.mult))
            v.tensor_tensor(n_g, n_g, cur[:, :, :], ALU.add)
        vector_block(fresh)
        scalar_fn(n_g, n_g, ACT.Tanh)

        def blend(v, ln):
            ln(v.tensor_tensor(cur[:, :, :], x[:, :, :], n_g, ALU.subtract))
            ln(v.tensor_tensor(cur[:, :, :], cur[:, :, :], z_g, ALU.mult))
            ln(v.tensor_tensor(cur[:, :, :], cur[:, :, :], n_g, ALU.add))
            v.tensor_tensor(x[:, :, :], x[:, :, :], cur[:, :, :], ALU.add)
        vector_block(blend)
        layernorm(x[:, :, :])

        R3 = D + 1
        wh_table = dram("cos_table", [N, R3])
        wh = acc[:, 0:NW * R3].rearrange("p (w f) -> p w f", f=R3)
        pc = sb("pc", [P, 12])
        copies((wts[0:D, 0:D], W_cos), (vecs[:, 0:D], row(b_cos)), (pc[:, 0:3], row(coeff_param)),
               (pc[:, 3:4], row(scale_param)))
        node_transpose([(lambda w: x[:, w, :], D, tT[0])])
        node_matmul([(window_of(tT[0], D), wts[0:D, 0:D])], D,
                    lambda v, w, n: nc.vector.tensor_tensor(
                        wh[:, w:w + n, 0:D], v, vecs[:, 0:D].unsqueeze(1).to_broadcast([P, n, D]), ALU.add))
        flat = acc[:, 0:NW * R3]
        accs = acc[:, NW * R3:NW * R3 + NW * D]
        sq3 = tmp[0:P, 0:NW * D].rearrange("p (w f) -> p w f", f=D)

        def norms(v, ln):
            ln(v.tensor_tensor(sq3, wh[:, :, 0:D], wh[:, :, 0:D], ALU.mult))
            v.tensor_reduce(small[:, 0, :], sq3, AX, ALU.add)
            ln(v.tensor_reduce(pc[:, 4:5], pc[:, 0:3], AX, ALU.max))
            ln(v.tensor_scalar(pc[:, 0:3], pc[:, 0:3], pc[:, 4:5], None, ALU.subtract))
            v.scalar_tensor_tensor(pc[:, 5:6], pc[:, 3:4], -1.0, pc[:, 3:4], ALU.mult, ALU.max)
        vector_block(norms)
        with nc.Block() as block:
            @block.scalar
            def _(act):
                nc.scalar.activation(wh[:, :, D], small[:, 0, :], ACT.Sqrt)
                nc.scalar.activation(pc[:, 8:11], pc[:, 0:3], ACT.Exp)
                link(act, nc.scalar.activation(pc[:, 6:7], pc[:, 5:6], ACT.Exp, scale=-1.0), act_ch)
                nc.scalar.activation(pc[:, 7:8], pc[:, 6:7], ACT.Ln, bias=1.0)

        def coeffs(v, ln):
            ln(v.tensor_reduce(pc[:, 4:5], pc[:, 8:11], AX, ALU.add))
            ln(v.reciprocal(pc[:, 5:6], pc[:, 4:5]))
            ln(v.tensor_scalar(pc[:, 8:11], pc[:, 8:11], pc[:, 5:6], None, ALU.mult))
            v.scalar_tensor_tensor(pc[:, 11:12], pc[:, 3:4], 0.0, pc[:, 7:8], ALU.max, ALU.add)
        vector_block(coeffs)
        c_pos, c_neg, c_own, c_scale = (pc[:, k:k + 1] for k in range(8, 12))
        copies((wh_table.rearrange("(w p) f -> p w f", p=P), wh))

        def cosine_pass():
            arrived = [sem(f"cos_rows{k}") for k in range(4)]
            weighed = sem("cos_weighed")
            hot, win_in, turned, hotT, src_rows, ch, logits, moved, summed, added = [sem(f"cos_{n}") for n in
                ("onehot", "window_rows", "turned", "onehotT", "source_rows", "chain", "similarity", "products",
                 "slot_sums", "added")]
            hotT_sb = arena[0:P, 0:G * P].rearrange("p (j e) -> p j e", e=P)
            win_rows = arena[0:P, 1000:1000 + G * R3].rearrange("p (j f) -> p j f", f=R3)
            prod = arena[0:P, 2000:2000 + G * D].rearrange("p (j f) -> p j f", f=D)
            mov = [arena[0:P, 3000 + b * 600:3000 + b * 600 + G * D].rearrange("p (j f) -> p j f", f=D) for b in range(2)]
            dot, nn, rn, sim, tp, tn, tw, we = [slotv[:, i, 0:G] for i in range(8)]
            own = ps[0:P, 6:8, 0:4 * R3].rearrange("p b (j f) -> p b j f", f=R3)
            vector_block(lambda v, ln: v.memset(accs, 0.0))
            with nc.Block() as block:
                @block.gpsimd
                def _(pool):
                    gather_engine("cos", pool, wh_table, cos_idx, R3, arrived, moved)

                @block.scalar
                def _(act):
                    def step(g, k):
                        act.wait_ge(turned, g + 1)
                        if after(g, 1):
                            act.wait_ge(src_rows, g)
                        nc.scalar.activation(hotT_sb.rearrange("p (b j) e -> p b (j e)", b=2), ps[0:P, 4:6, 0:4 * P],
                                             ACT.Copy).then_inc(hotT, 1)
                    run(act, step, 0)

                @block.tensor
                def _(pe):
                    def step(g, k):
                        if not isinstance(g, int) or g < NG:
                            pe.wait_ge(hot, g + 1)
                            if after(g, 1):
                                pe.wait_ge(hotT, g)
                            for j in range(G):
                                last = nc.tensor.transpose(ps[0:P, 4 + j // 4, (j % 4) * P:(j % 4 + 1) * P],
                                                           onehot[:, k, j, :], ident[0:P, 0:P])
                            last.then_inc(turned, 1)
                            pe.wait_ge(hotT, g + 1)
                            pe.wait_ge(win_in, g + 1)
                            if after(g, 1):
                                pe.wait_ge(logits, g)
                            for j in range(G):
                                last = nc.tensor.matmul(ps[0:P, 6 + j // 4, (j % 4) * R3:(j % 4 + 1) * R3],
                                                        hotT_sb[:, j, :], win_rows[:, j, :], start=True, stop=True)
                            last.then_inc(src_rows, 1)
                        if after(g, 1):
                            b = (k + 3) % 4
                            pe.wait_ge(moved, g)
                            if after(g, 3):
                                pe.wait_ge(added, (g - 2) * G)
                            for j in range(G):
                                last = nc.tensor.matmul(ps[0:P, b % 2, j * D:(j + 1) * D], onehot[:, b, j, :],
                                                        mov[b % 2][:, j, :], start=True, stop=True)
                            last.then_inc(summed, 1)
                    run(pe, step, 1)

                @block.vector
                def _(dve):
                    v = nc.vector

                    def step(g, k):
                        q = k % 2
                        if not isinstance(g, int) or g < NG:
                            if after(g, 4):
                                dve.wait_ge(summed, g - 3)
                            to_rows(v, onehot[:, k, :, :], sloc, g).then_inc(hot, 1)
                            w = windows(g, cos_win_row)
                            if after(g, 1):
                                dve.wait_ge(src_rows, g)
                            for j in range(G):
                                last = v.tensor_copy(win_rows[:, j, :], flat[:, ds(w[j] * R3, R3)])
                            last.then_inc(win_in, 1)
                        if after(g, 2):
                            w = windows(g - 2, cos_win_row)
                            dve.wait_ge(summed, g - 1)
                            for j in range(G):
                                if after(g, 3) or j:
                                    dve.wait_ge(added, (g - 2) * G + j)
                                a = accs[:, ds(w[j] * D, D)]
                                v.tensor_tensor(a, a, ps[0:P, k % 2, j * D:(j + 1) * D], ALU.add).then_inc(added, 1)
                        if not isinstance(g, int) or g < NG:
                            dve.wait_ge(src_rows, g + 1)
                            dve.wait_ge(arrived[k], full(g, k))
                            n = [g * 8]

                            def ln(ins, wait=True):
                                n[0] = n[0] + 1
                                ins.then_inc(ch, 1)
                                if wait:
                                    dve.wait_ge(ch, n[0])
                            gk = rows_of(k, R3)
                            gb = gk.rearrange("p (b j) f -> p b j f", b=2)
                            ln(v.tensor_tensor(prod.rearrange("p (b j) f -> p b j f", b=2), gb[:, :, :, 0:D],
                                               own[:, :, :, 0:D], ALU.mult), wait=False)
                            v.tensor_tensor(nn.rearrange("p (b j) -> p b j", b=2), gb[:, :, :, D],
                                            own[:, :, :, D], ALU.mult).then_inc(logits, 1)
                            dve.wait_ge(logits, g + 1)
                            ln(v.tensor_scalar(nn, nn, SIM_EPS, None, ALU.max))
                            ln(v.reciprocal(rn, nn), wait=False)
                            ln(v.tensor_reduce(dot, prod, AX, ALU.add))
                            ln(v.tensor_tensor(sim, dot, rn, ALU.mult))
                            ln(v.tensor_scalar(tp, sim, 0.0, c_pos, ALU.max, ALU.mult), wait=False)
                            ln(v.tensor_scalar(tn, sim, 0.0, c_neg, ALU.min, ALU.mult))
                            ln(v.tensor_tensor(tw, tp, tn, ALU.add))
                            if after(g, 1):
                                dve.wait_ge(moved, g)
                            v.tensor_tensor(we, tw, base_w[:, ds(g * G, G)], ALU.mult).then_inc(weighed, 1)
                            dve.wait_ge(weighed, g + 1)
                            if after(g, 2):
                                dve.wait_ge(summed, g - 1)
                            v.tensor_tensor(mov[q], gk[:, :, 0:D], bf(we, D), ALU.mult).then_inc(moved, 1)
                    run(dve, step, 2)

        cosine_pass()

        def gathered(v, ln):
            t3 = tmp[0:P, 0:NW * D].rearrange("p (w f) -> p w f", f=D)
            ln(v.tensor_scalar(t3, wh[:, :, 0:D], c_own, None, ALU.mult))
            ln(v.tensor_tensor(t3, t3, accs.rearrange("p (w f) -> p w f", f=D), ALU.add))
            v.scalar_tensor_tensor(x[:, :, :], t3, c_scale, x[:, :, :], ALU.mult, ALU.add)
        vector_block(gathered)
        layernorm(x[:, :, :])
        copies((out.rearrange("(w p) f -> p w f", p=P), x[:, :, :]))


_INS = ['x', 'src', 'dst', 'edge_type_8', 'edge_weight', 'edge_weight_n2',
        'L0_gnn_W1', 'L0_gnn_as1', 'L0_gnn_ad1', 'L0_gnn_b1', 'L0_gnn_g1', 'L0_gnn_be1',
        'L0_gnn_W2', 'L0_gnn_as2', 'L0_gnn_ad2', 'L0_gnn_b2', 'L0_gnn_g2', 'L0_gnn_be2',
        'L0_gnn_W3', 'L0_gnn_as3', 'L0_gnn_ad3', 'L0_gnn_b3',
        'L1_gnn_W_self', 'L1_gnn_W_neigh', 'L1_gnn_b',
        'L2_gnn_edge_matrix', 'L2_gnn_w_ih', 'L2_gnn_w_hh', 'L2_gnn_b_ih', 'L2_gnn_b_hh',
        'L3_gnn_W', 'L3_gnn_b', 'L3_gnn_deg_coeff', 'L3_gnn_coeff_param', 'L3_gnn_scale_param']
_OUTS = [((N, D), 'float32')]


def kernel(**inputs):
    import numpy as _np
    import concourse.bacc as _bacc
    from concourse import mybir as _mybir
    from concourse.bass_utils import run_bass_kernel_spmd as _run

    nc = _bacc.Bacc("TRN2", target_bir_lowering=False, num_devices=1)
    arrays, args = {}, []
    for name in _INS:
        a = _np.ascontiguousarray(inputs[name])
        arrays[f"in_{name}_dram"] = a
        args.append(nc.dram_tensor(f"in_{name}_dram", a.shape, _mybir.dt.from_np(a.dtype), kind="ExternalInput").ap())
    for i, (shape, dtype) in enumerate(_OUTS):
        dt = _mybir.dt.from_np(_np.dtype(dtype))
        args.append(nc.dram_tensor(f"out_{i}_dram", shape, dt, kind="ExternalOutput").ap())
    gnn_kernel(nc, *args)
    r = _run(nc, [arrays], core_ids=[0])
    return r.results[0]["out_0_dram"]
```
